# Optimizing a Trainium2 kernel written in Bass

```python
import numpy as np
import jax
import jax.numpy as jnp

def _softmax(x, axis=-1):
    return jax.nn.softmax(x, axis=axis)

def _gelu(x):
    return jax.nn.gelu(x, approximate=True)

def _silu(x):
    return jax.nn.silu(x)

def _sigmoid(x):
    return jax.nn.sigmoid(x)

def _layernorm(x, axis=-1, eps=1e-05):
    m = jnp.mean(x, axis=axis, keepdims=True)
    v = jnp.var(x, axis=axis, keepdims=True)
    return (x - m) / jnp.sqrt(v + eps)

def _scatter_add(tgt, idx, src, axis=0):
    return tgt.at[idx].add(src)

def _segment_sum(src, seg, n):
    return jax.ops.segment_sum(src, seg, n)
kernel_name = 'mk_adj_preln_d2_adj_r2_67130c'

def setup_inputs(seed: int=0):
    np.random.seed(seed)
    _w = jnp.asarray

    def _rec_inputs():
        import jax
        import jax.numpy as jnp
        _gk = jax.random.key(seed)
        x = -0.000929 + 1 * jax.random.normal(jax.random.fold_in(_gk, 1), (8, 2048, 64), jnp.float32)
        _a = jax.random.bernoulli(jax.random.fold_in(_gk, 2), 0.00195312, (8, 2048, 2048))
        _a = jnp.logical_or(_a, jnp.swapaxes(_a, -1, -2))
        _a = jnp.logical_or(_a, jnp.eye(2048, dtype=bool))
        _af = _a.astype(jnp.float32)
        _af = _af * jax.random.uniform(jax.random.fold_in(_gk, 3), (8, 2048, 2048), jnp.float32, 0.05, 1)
        adj = _af
        return (x, adj)
    x, adj = _rec_inputs()

    def _L0_gnn_setup():
        import jax, jax.numpy as jnp
        import numpy as np
        B, N, C, R = (4, 2048, 64, 16)
        EPS = 1e-12
        key = jax.random.key(seed)
        k_x, k_w, k_u = jax.random.split(key, 3)
        x = jax.random.normal(k_x, (B, N, C), dtype=jnp.float32)
        W = jax.random.uniform(k_w, (B, N, N), dtype=jnp.float32)
        U = 0.01 * jax.random.normal(k_u, (N, R), dtype=jnp.float32)
        w_scale = jnp.asarray(1.0, dtype=jnp.float32)
        return {'x': x, 'W': W, 'U': U, 'w_scale': w_scale}
    _L0_gnn_all = _L0_gnn_setup()
    _L0_gnn_in = {k: v for k, v in _L0_gnn_all.items() if k in ('U', 'w_scale')}
    del _L0_gnn_all

    def _L1_gnn_setup():
        import jax, jax.numpy as jnp
        import numpy as np
        B, N, D, L = (128, 325, 64, 3)
        EPS = 1e-05
        key = jax.random.key(seed)
        k = jax.random.split(key, 6)
        X = jax.random.normal(k[0], (B, N, D), dtype=jnp.float32)
        adj = jax.random.uniform(k[1], (B, N, N), dtype=jnp.float32)
        limit = float(np.sqrt(6.0 / (D + D)))
        W = jax.random.uniform(k[2], (L, D, D), minval=-limit, maxval=limit, dtype=jnp.float32)
        b = jnp.zeros((L, D), dtype=jnp.float32)
        gamma = jnp.ones((L, D), dtype=jnp.float32)
        beta = jnp.zeros((L, D), dtype=jnp.float32)
        return {'X': X, 'adj': adj, 'W': W, 'b': b, 'gamma': gamma, 'beta': beta}
    _L1_gnn_all = _L1_gnn_setup()
    _L1_gnn_in = {k: v for k, v in _L1_gnn_all.items() if k in ('W', 'b', 'gamma', 'beta')}
    del _L1_gnn_all
    return {'x': x, 'adj': adj, 'L0_gnn_U': _L0_gnn_in['U'], 'L0_gnn_w_scale': _L0_gnn_in['w_scale'], 'L1_gnn_W': _L1_gnn_in['W'], 'L1_gnn_b': _L1_gnn_in['b'], 'L1_gnn_gamma': _L1_gnn_in['gamma'], 'L1_gnn_beta': _L1_gnn_in['beta']}

def reference(x, adj, L0_gnn_U, L0_gnn_w_scale, L1_gnn_W, L1_gnn_b, L1_gnn_gamma, L1_gnn_beta):
    import jax
    import jax.numpy as jnp

    def _L0_gnn_ref(x, W, U, w_scale):
        import jax, jax.numpy as jnp
        import numpy as np
        B, N, C, R = (4, 2048, 64, 16)
        EPS = 1e-12
        Ws = 0.5 * (W + jnp.swapaxes(W, -1, -2))
        A = jax.nn.sigmoid(U @ U.T)
        K = Ws * A[None, :, :]
        deg = jnp.maximum(K.sum(axis=-1), EPS)
        d = jax.lax.rsqrt(deg)
        K = K * d[:, :, None] * d[:, None, :]
        return w_scale * jnp.einsum('bnm,bmc->bnc', K, x)

    def _L1_gnn_ref(X, adj, W, b, gamma, beta):
        import jax, jax.numpy as jnp
        import numpy as np
        B, N, D, L = (128, 325, 64, 3)
        EPS = 1e-05
        h = X
        for l in range(L):
            hw = jnp.einsum('bnd,de->bne', h, W[l])
            agg = jnp.einsum('bji,bjd->bid', adj, hw) + b[l]
            y = agg + h
            mu = jnp.mean(y, axis=-1, keepdims=True)
            var = jnp.mean(jnp.square(y - mu), axis=-1, keepdims=True)
            yn = (y - mu) * jax.lax.rsqrt(var + EPS) * gamma[l] + beta[l]
            h = jax.nn.relu(yn)
        return h
    h = jnp.maximum(_layernorm(x, axis=-1), 0.0)
    x = x + _L0_gnn_ref(h, adj, L0_gnn_U, L0_gnn_w_scale)
    h = jnp.maximum(_layernorm(x, axis=-1), 0.0)
    x = x + _L1_gnn_ref(h, adj, L1_gnn_W, L1_gnn_b, L1_gnn_gamma, L1_gnn_beta)
    return x

_drawn_inputs = setup_inputs


def setup_inputs(seed=0):
    import zlib

    import numpy as np

    out = dict(_drawn_inputs(seed))
    spreads = {'L1_gnn_b': (0.0, 0.1), 'L1_gnn_gamma': (1.0, 0.2), 'L1_gnn_beta': (0.0, 0.1)}
    factors = {'L0_gnn_U': 64.0}
    for name, (base, spread) in spreads.items():
        noise = np.random.default_rng([zlib.crc32(name.encode()), seed]).standard_normal(out[name].shape)
        drawn = base * np.exp(spread * noise) if base else spread * noise
        out[name] = jnp.asarray(drawn.astype(out[name].dtype))
    for name, factor in factors.items():
        out[name] = (out[name] * factor).astype(out[name].dtype)
    return out
```

```python
import concourse.bass as bass
from concourse import mybir
from contextlib import ExitStack


def adjacency_mixer_kernel(nc, x, adj, U, w_scale, W, bias, gamma, beta, out):
    fp32 = mybir.dt.float32
    bf16 = mybir.dt.bfloat16
    ALU = mybir.AluOpType
    ACT = mybir.ActivationFunctionType
    AX = mybir.AxisListType

    B, N, C = x.shape
    R = U.shape[1]
    L = W.shape[0]
    P = 128
    T = N // P
    CH = 512
    NC = N // CH
    TC = CH // P
    HT = T // 2
    HC = HT * C
    DEG_EPS = 1e-12
    LN_EPS = 1e-5

    BUILD = [(j, c) for j in range(T) for c in range(j // TC + 1)]
    NB = len(BUILD)
    NORMS = 4 + 2 * L
    OUTS = 2 + 2 * L

    def build_cols(j, c):
        return min((c + 1) * TC, j + 1) * P - c * CH

    def strip(j):
        return j * (j + 1) // 2 * P

    def flipped(i, c):
        return list(range(max(TC * c, i + 1), TC * (c + 1)))

    PIECES = []
    for half in range(2):
        for i in range(T):
            for c in range(half * NC // 2, (half + 1) * NC // 2):
                if TC * c <= i:
                    PIECES.append((half, i, c, False))
                if flipped(i, c):
                    PIECES.append((half, i, c, True))
    FLIPS = [(i, c) for _, i, c, turned in PIECES if turned]
    NF = len(FLIPS)
    RING = 4
    SLOTS = 2

    ctx = ExitStack()
    with ctx:
        def sb(name, shape, dt=fp32):
            return ctx.enter_context(nc.sbuf_tensor(name, shape, dt))

        def sem(name):
            return ctx.enter_context(nc.semaphore(name))

        Wt = sb("adjacency", [P, T, N])
        Kt = sb("k_lower", [P, strip(T)])
        ul = sb("u_left", [P, N], bf16)
        ur = sb("u_right", [P, N], bf16)
        xr = sb("x_residual", [P, T * C])
        hA = sb("h_a", [P, T * C])
        hB = sb("h_b", [P, T * C])
        G = sb("product_out", [P, CH])
        ident = sb("ident", [P, P])
        wl = sb("weights_twice", [P, L, 2 * C])
        bs = sb("bias_rows", [P, L, C])
        gs = sb("gamma_rows", [P, L, C])
        be = sb("beta_rows", [P, L, C])
        ws = sb("w_scale_col", [P, 1])
        ones = sb("ones", [P, 32])
        expo = sb("minus_half", [P, T])
        rows = sb("row_sums", [P, T, NC])
        deg = sb("degree", [P, T])
        dis = sb("degree_rsqrt", [P, T])
        dout = sb("degree_out", [P, T])
        rd = sb("norm_times_degree", [P, T])
        mean = sb("mean", [P, HT])
        var = sb("variance", [P, 2, HT])
        rstd = sb("rstd", [P, 2, HT])

        KIND = 8
        cat = [Kt[:, m * T * P:(m + 1) * T * P].rearrange("p (t k) -> p t k", t=T) for m in range(2)]
        u_in = hA[:, 0:T * R].rearrange("p (t r) -> p t r", t=T)
        u_rest = [hA[:, (1 + m) * T * R:(2 + m) * T * R].rearrange("p (t r) -> p t r", t=T) for m in range(2)]
        u_part = [hB[:, m * T * R // 2:(m + 1) * T * R // 2].bitcast(bf16).rearrange("p (t r) -> p t r", t=T)
                  for m in range(3)]

        h1 = Kt[:, 0:T * C]
        turned_sb = hA[:, :].rearrange("p (s n) -> p s n", s=SLOTS)

        acc = ctx.enter_context(nc.psum_tensor("acc", [P, 2, CH], fp32))
        ring = ctx.enter_context(nc.psum_tensor("ring", [P, RING, CH], fp32))
        col = ctx.enter_context(nc.psum_tensor("column_sums", [P, CH], fp32))
        yps = ctx.enter_context(nc.psum_tensor("y_psum", [P, CH], fp32))

        w_in = [sem(f"strip_in_{j}") for j in range(T)]
        u_loaded = sem("u_loaded")
        const_in = sem("const_in")
        x_in = sem("x_in")
        out_stored = sem("out_stored")
        wl_zeroed = sem("wl_zeroed")
        ident_made = sem("ident_made")
        ones_made = sem("ones_made")
        u_split = sem("u_split")
        u_turned = sem("u_turned")
        u_ready = sem("u_ready")
        gate_in = sem("gate_in")
        gated = sem("gated")
        turned_in = sem("turned_in")
        summed = sem("summed")
        k_made = sem("k_made")
        cols_summed = sem("cols_summed")
        cols_out = sem("cols_out")
        cols_turned = sem("cols_turned")
        deg_made = sem("deg_made")
        dis_made = sem("dis_made")
        dh_made = sem("dh_made")
        flip_in = sem("flip_in")
        flip_out = sem("flip_out")
        flip_used = sem("flip_used")
        acc_done = sem("acc_done")
        g_out = sem("g_out")
        y_done = sem("y_done")
        centred = sem("centred")
        squared = sem("squared")
        var_made = sem("var_made")
        rstd_made = sem("rstd_made")
        h_made = sem("h_made")
        strip_free = sem("strip_free")
        result = sem("result")
        step = sem("vector_step")

        def half(ap, p):
            return ap[:, p * HC:(p + 1) * HC]

        def tiles(ap):
            return ap.rearrange("p (t c) -> p t c", c=C)

        def over_c(ap):
            return ap.unsqueeze(2).broadcast_to([P, HT, C])

        def over_t(ap):
            return ap.unsqueeze(1).broadcast_to([P, HT, C])

        reads = [h1, hA[:, :], hB[:, :]]
        writes = [hA[:, :], hB[:, :], hA[:, :]]

        block = ctx.enter_context(nc.Block())

        @block.sync
        def _(sp):
            def load_x(b):
                sp.dma_start(tiles(xr[:, :]), x[b].rearrange("(t p) c -> p t c", p=P)).then_inc(x_in, 16)

            def load_strip(b, j):
                sp.dma_start(Wt[:, j, :], adj[b, j * P:(j + 1) * P, :]).then_inc(w_in[j], 16)

            sp.dma_start(u_in, U.rearrange("(t p) r -> p t r", p=P)).then_inc(u_loaded, 16)
            load_strip(0, 0)
            for q in range(2):
                sp.wait_ge(wl_zeroed, 1)
                sp.dma_start(wl[q * C:(q + 1) * C, :, q * C:(q + 1) * C], W.rearrange("l d e -> d l e")).then_inc(const_in, 16)
            for rows_sb, src in ((bs, bias), (gs, gamma), (be, beta)):
                sp.dma_start(rows_sb[:, :, :], src.partition_broadcast(P)).then_inc(const_in, 16)
            sp.dma_start(ws[:, :], w_scale.partition_broadcast(P)).then_inc(const_in, 16)
            load_x(0)
            for j in range(1, T):
                load_strip(0, j)

            def store(b):
                sp.wait_ge(result, 2 * b + 2)
                sp.dma_start(out[b].rearrange("(t p) c -> p t c", p=P), tiles(hA[:, :])).then_inc(out_stored, 16)

            with sp.Fori(0, B - 1) as b:
                for j in range(T):
                    if j < T - 1:
                        sp.wait_ge(strip_free, (T - 1) * b + j + 1)
                    else:
                        sp.wait_ge(acc_done, OUTS * (b + 1))
                    load_strip(b + 1, j)
                store(b)
                load_x(b + 1)
            store(B - 1)
            sp.wait_ge(out_stored, 16 * B)

        @block.tensor
        def _(pe):
            def product(bank, h, j, c):
                o = C * (c % 2)
                return nc.tensor.matmul(acc[o:o + C, bank, :], h[:, j * C:(j + 1) * C],
                                        Wt[:, j, c * CH:(c + 1) * CH], start=(j == 0), stop=(j == T - 1))

            def layer_step(b, l, j, halves=(0, 1)):
                for p in halves:
                    if j == 0:
                        pe.wait_ge(g_out, OUTS * b + 2 * l + p + 1)
                    if j % HT == 0:
                        pe.wait_ge(h_made, 2 * L * b + 2 * l + j // HT + 1)
                    for c in (2 * p, 2 * p + 1):
                        m = product(p, reads[l], j, c)
                    if j == T - 1:
                        m.then_inc(acc_done, 1)
                return m

            def leave(b, n):
                pe.wait_ge(g_out, OUTS * b + n + 1)
                pe.wait_ge(var_made, NORMS * b + n + 2)
                if n == 0:
                    pe.wait_ge(deg_made, b + 1)
                rhs = ident[:, :] if n < 2 else wl[:, (n - 2) // 2, :]
                by_chunk = yps[:, :].rearrange("p (a k c) -> p a k c", a=2, c=C)
                for k in range(TC):
                    m = nc.tensor.matmul(by_chunk[:, :, k, :], G[:, k * P:(k + 1) * P], rhs, start=True, stop=True)
                m.then_inc(y_done, 1)

            def build_unit(b, u):
                j, c = BUILD[u]
                n = build_cols(j, c)
                if not isinstance(b, int) or NB * b + u >= 2:
                    pe.wait_ge(k_made, NB * b + u - 1)
                if u == 0:
                    pe.wait_ge(flip_out, NF * b) if not isinstance(b, int) else None
                nc.tensor.matmul(ring[:, u % 2, 0:n], ul[:, j * P:(j + 1) * P], ur[:, c * CH:c * CH + n],
                                 start=True, stop=True).then_inc(gate_in, 1)
                if c == 0:
                    pe.wait_ge(w_in[j], 16 * (b + 1))
                if not isinstance(b, int) or NB * b + u >= 2:
                    pe.wait_ge(summed, NB * b + u - 1)
                for k in range(n // P):
                    m = nc.tensor.transpose(ring[:, 2 + u % 2, k * P:(k + 1) * P],
                                            Wt[:, c * TC + k, j * P:(j + 1) * P], ident[:, :])
                m.then_inc(turned_in, 1)

            def column_sums(b, u):
                j, c = BUILD[u]
                n = min(build_cols(j, c), (j - c * TC) * P)
                if n == 0:
                    return
                pe.wait_ge(k_made, NB * b + u + 1)
                m = nc.tensor.matmul(col[32 * c:32 * c + 32, 0:n], ones[:, :],
                                     Kt[:, strip(j) + c * CH:strip(j) + c * CH + n],
                                     start=(j == c * TC + 1), stop=(j == T - 1), skip_group_check=True)
                if u == NB - 1:
                    m.then_inc(cols_summed, 1)

            def build_tail(b):
                column_sums(b, NB - 2)
                column_sums(b, NB - 1)
                pe.wait_ge(cols_out, 2 * b + 2)
                pe.wait_ge(var_made, NORMS * b + 2)
                by_chunk = yps[:, 0:T].rearrange("p (c k) -> p c k", k=TC)
                for k in range(TC):
                    n = NC if k < TC - 1 else NC - 1
                    m = nc.tensor.matmul(by_chunk[:, 0:n, k], G[0:32 * n, k * P:(k + 1) * P],
                                         ident[0:32 * n, 0:32 * (n - 1) + 1:32], start=True, stop=True)
                m.then_inc(cols_turned, 1)

            def flip(b, v):
                i, c = FLIPS[v]
                if v == 0:
                    pe.wait_ge(k_made, NB * (b + 1))
                if v >= RING:
                    pe.wait_ge(flip_out, NF * b + v - RING + 1)
                for k, j in enumerate(flipped(i, c)):
                    m = nc.tensor.transpose(ring[:, v % RING, k * P:(k + 1) * P],
                                            Kt[:, strip(j) + i * P:strip(j) + (i + 1) * P], ident[:, :])
                m.then_inc(flip_in, 1)

            def k_product(b):
                for v in range(RING - 1):
                    flip(b, v)
                pe.wait_ge(dh_made, b + 1)
                v = 0
                first = set()
                for n, (p, i, c, turned) in enumerate(PIECES):
                    o = C * (c % 2)
                    if turned:
                        if v + RING - 1 < NF:
                            flip(b, v + RING - 1)
                        pe.wait_ge(flip_out, NF * b + v + 1)
                        lo = flipped(i, c)[0] * P - c * CH
                        rhs, a, e = turned_sb[:, v % SLOTS, 0:CH - lo], lo, CH
                        v += 1
                    else:
                        a, e = 0, min(CH, (i + 1) * P - c * CH)
                        rhs = Kt[:, strip(i) + c * CH:strip(i) + c * CH + e]
                    m = nc.tensor.matmul(acc[o:o + C, p, a:e], hB[:, i * C:(i + 1) * C], rhs,
                                         start=(c not in first), stop=(i == T - 1), skip_group_check=True)
                    first.add(c)
                    if turned:
                        m.then_inc(flip_used, 1)
                    elif n + 1 == len(PIECES) or PIECES[n + 1][0] != p:
                        m.then_inc(acc_done, 1)
                    if (p, i, c) == (1, 1, NC - 1) and turned:
                        leave(b, 0)

            def full_layer(b, l):
                for j in range(T):
                    layer_step(b, l, j, (0,))
                    if j == 2:
                        leave(b, 2 * l + 1)
                for j in range(T):
                    layer_step(b, l, j, (1,))
                    if j == 2:
                        leave(b, 2 * l + 2)

            def last_layer_step(b, j):
                if j == 2:
                    for i in range(3):
                        layer_step(b, L - 1, i, (0,))
                    leave(b, 2 * L - 1)
                    for i in range(3):
                        layer_step(b, L - 1, i, (1,)).then_inc(strip_free, 1)
                elif j == T - 1:
                    layer_step(b, L - 1, j)
                elif j > 2:
                    layer_step(b, L - 1, j).then_inc(strip_free, 1)

            def window(b):
                at = 0
                u = 0
                for s in range(T):
                    lead = min(T, 4 + 3 * s // 2)
                    while at < lead:
                        last_layer_step(b, at)
                        at += 1
                    while u < NB and BUILD[u][0] == s:
                        build_unit(b + 1, u)
                        if u >= 2:
                            column_sums(b + 1, u - 2)
                        u += 1
                    if s == 9:
                        leave(b, 2 * L)
                    if s == 11:
                        leave(b, 2 * L + 1)
                build_tail(b + 1)

            pe.wait_ge(ident_made, 2)
            for m in range(2):
                pe.wait_ge(u_split, m + 1)
                for q in range(NC):
                    if m == 1:
                        pe.wait_ge(u_ready, q + 1)
                    for k in range(TC):
                        t = nc.tensor.transpose(ring[:, q, k * P:(k + 1) * P], cat[m][:, q * TC + k, :], ident[:, :])
                    t.then_inc(u_turned, 1)
            pe.wait_ge(u_ready, 2 * NC)
            pe.wait_ge(ones_made, 1)
            for u in range(NB):
                build_unit(0, u)
                if u >= 2:
                    column_sums(0, u - 2)
            build_tail(0)

            with pe.Fori(0, B - 1) as b:
                k_product(b)
                for l in range(L - 1):
                    full_layer(b, l)
                window(b)
            k_product(B - 1)
            for l in range(L - 1):
                full_layer(B - 1, l)
            for j in range(T):
                last_layer_step(B - 1, j)
            leave(B - 1, 2 * L)
            leave(B - 1, 2 * L + 1)

        @block.scalar
        def _(act):
            def gate(b, u):
                j, c = BUILD[u]
                n = build_cols(j, c)
                act.wait_ge(gate_in, NB * b + u + 1)
                nc.scalar.activation(ring[:, u % 2, 0:n], ring[:, u % 2, 0:n], ACT.Sigmoid).then_inc(gated, 1)

            def square(b, n, src):
                act.wait_ge(centred, NORMS * b + n + 1)
                if n or not isinstance(b, int):
                    act.wait_ge(var_made, NORMS * b + n)
                nc.scalar.activation(yps[:, :], src, ACT.Square).then_inc(squared, 1)

            def product_out(b, n):
                act.wait_ge(acc_done, OUTS * b + n + 1)
                if n == 0:
                    act.wait_ge(cols_turned, b + 1)
                else:
                    act.wait_ge(y_done, OUTS * b + n)
                nc.scalar.activation(G[:, :], acc[:, n % 2, :], ACT.Copy).then_inc(g_out, 1)

            def cols_to_sbuf(b):
                act.wait_ge(cols_summed, b + 1)
                if not isinstance(b, int):
                    act.wait_ge(y_done, OUTS * b)
                nc.scalar.activation(G[0:96, :], col[0:96, :], ACT.Copy).then_inc(cols_out, 1)
                nc.scalar.activation(G[96:128, 0:CH - P], col[96:128, 0:CH - P], ACT.Copy).then_inc(cols_out, 1)

            def flip_to_sbuf(b, v):
                n = len(flipped(*FLIPS[v])) * P
                act.wait_ge(flip_in, NF * b + v + 1)
                if v == 0 and not isinstance(b, int):
                    act.wait_ge(out_stored, 16 * b)
                if v == 0 and isinstance(b, int) and b > 0:
                    act.wait_ge(out_stored, 16 * b)
                if v >= SLOTS:
                    act.wait_ge(flip_used, NF * b + v - SLOTS + 1)
                nc.scalar.activation(turned_sb[:, v % SLOTS, 0:n], ring[:, v % RING, 0:n], ACT.Copy).then_inc(flip_out, 1)

            half_flips = sum(1 for p, _, _, turned in PIECES if turned and p == 0)

            def k_and_layers(b):
                for v in range(NF):
                    if v == half_flips + 2:
                        product_out(b, 0)
                    if v == half_flips + 8:
                        square(b, 2, half(h1, 0))
                    flip_to_sbuf(b, v)
                product_out(b, 1)
                square(b, 3, half(h1, 1))
                for l in range(L - 1):
                    for p in range(2):
                        product_out(b, 2 + 2 * l + p)
                        square(b, 4 + 2 * l + p, half(writes[l], p))

            def last_out(b, p):
                product_out(b, 2 * L + p)
                square(b, 2 + 2 * L + p, half(writes[L - 1], p))

            for u in range(NB):
                gate(0, u)
                if u in (4, 6):
                    square(0, (u - 4) // 2, half(hB, (u - 4) // 2))
            cols_to_sbuf(0)
            with act.Fori(0, B - 1) as b:
                k_and_layers(b)
                for u in range(NB):
                    gate(b + 1, u)
                    if BUILD[u] == (9, 1):
                        product_out(b, 2 * L)
                    if BUILD[u] == (10, 1):
                        square(b, 2 + 2 * L, half(writes[L - 1], 0))
                    if BUILD[u] == (11, 1):
                        product_out(b, 2 * L + 1)
                    if BUILD[u] == (12, 1):
                        square(b, 3 + 2 * L, half(writes[L - 1], 1))
                for p in range(2):
                    square(b + 1, p, half(hB, p))
                cols_to_sbuf(b + 1)
            k_and_layers(B - 1)
            last_out(B - 1, 0)
            last_out(B - 1, 1)

        @block.gpsimd
        def _(pool):
            pool.memset(wl[:, :, :], 0.0).then_inc(wl_zeroed, 1)
            pool.memset(ident[:, :], 0.0).then_inc(ident_made, 1)
            pool.wait_ge(ident_made, 1)
            pool.affine_select(out=ident[:, :], in_=ident[:, :], compare_op=ALU.not_equal, fill=1.0,
                               base=0, pattern=[[-1, P]], channel_multiplier=1).then_inc(ident_made, 1)
            pool.wait_ge(ones_made, 1)

            def root(b, n):
                pool.wait_ge(var_made, NORMS * b + n + 1)
                nc.gpsimd.tensor_tensor(rstd[:, n % 2, :], var[:, n % 2, :], expo[:, 0:HT], ALU.pow).then_inc(rstd_made, 1)

            def degree_root(b):
                pool.wait_ge(deg_made, b + 1)
                nc.gpsimd.tensor_tensor(dis[:, :], deg[:, :], expo[:, :], ALU.pow).then_inc(dis_made, 1)

            with pool.Fori(0, B) as b:
                root(b, 0)
                root(b, 1)
                degree_root(b)
                for n in range(2, NORMS):
                    root(b, n)

        STEPS_BATCH = 3 * NORMS + 4 + 2 * 2 + 2 * L * 5

        @block.vector
        def _(dve):
            steps = [0]
            steps_before = [0]

            def link(instruction):
                steps[0] += 1
                instruction.then_inc(step, 1)
                dve.wait_ge(step, steps[0] + steps_before[0])

            def add_transposed(b, u):
                j, c = BUILD[u]
                n = build_cols(j, c)
                at = strip(j) + c * CH
                dve.wait_ge(w_in[j], 16 * (b + 1))
                dve.wait_ge(turned_in, NB * b + u + 1)
                nc.vector.tensor_tensor(Kt[:, at:at + n], Wt[:, j, c * CH:c * CH + n], ring[:, 2 + u % 2, 0:n],
                                        ALU.add).then_inc(summed, 1)

            def times_gate(b, u):
                j, c = BUILD[u]
                n = build_cols(j, c)
                at = strip(j) + c * CH
                dve.wait_ge(summed, NB * b + u + 1)
                dve.wait_ge(gated, NB * b + u + 1)
                nc.vector.scalar_tensor_tensor(out=Kt[:, at:at + n], in0=Kt[:, at:at + n], scalar=1.0,
                                               in1=ring[:, u % 2, 0:n], op0=ALU.mult, op1=ALU.mult,
                                               accum_out=rows[:, j, c:c + 1]).then_inc(k_made, 1)

            def centre(b, n, src, dst):
                link(nc.vector.tensor_reduce(mean[:, :], tiles(src), AX.X, ALU.add))
                link(nc.vector.tensor_scalar(mean[:, :], mean[:, :], 1.0 / C, None, ALU.mult))
                nc.vector.tensor_tensor(tiles(dst), tiles(src), over_c(mean[:, :]), ALU.subtract).then_inc(centred, 1)

            def variance(b, n):
                dve.wait_ge(squared, NORMS * b + n + 1)
                link(nc.vector.tensor_reduce(var[:, n % 2, :], tiles(yps[:, :]), AX.X, ALU.add))
                nc.vector.tensor_scalar(var[:, n % 2, :], var[:, n % 2, :], 1.0 / C, LN_EPS, ALU.mult, ALU.add)\
                  .then_inc(var_made, 1)

            def first_norm(b, p):
                dve.wait_ge(x_in, 16 * (b + 1))
                if p == 0 and not isinstance(b, int):
                    dve.wait_ge(acc_done, OUTS * b)
                centre(b, p, half(xr, p), half(hB, p))

            def degrees(b):
                dve.wait_ge(k_made, NB * (b + 1))
                link(nc.vector.tensor_reduce(deg[:, :], rows[:, :, :], AX.X, ALU.add))
                dve.wait_ge(cols_turned, b + 1)
                link(nc.vector.tensor_tensor(deg[:, 0:T - 1], deg[:, 0:T - 1], yps[:, 0:T - 1], ALU.add))
                nc.vector.tensor_scalar(deg[:, :], deg[:, :], 0.5, DEG_EPS, ALU.mult, ALU.max).then_inc(deg_made, 1)
                dve.wait_ge(dis_made, b + 1)
                dve.wait_ge(rstd_made, NORMS * b + 2)
                link(nc.vector.tensor_tensor(rd[:, :], dis[:, :], rstd[:, :, :].rearrange("p a t -> p (a t)"), ALU.mult))
                link(nc.vector.tensor_scalar(dout[:, :], dis[:, :], ws[:, 0:1], 0.5, ALU.mult, ALU.mult))
                nc.vector.scalar_tensor_tensor(out=tiles(hB[:, :]), in0=tiles(hB[:, :]), scalar=0.0,
                                               in1=rd[:, :].unsqueeze(2).broadcast_to([P, T, C]),
                                               op0=ALU.max, op1=ALU.mult).then_inc(dh_made, 1)

            def first_residual(b, p):
                dve.wait_ge(y_done, OUTS * b + p + 1)
                ys, xs, hs = tiles(yps[:, :]), half(xr, p), half(h1, p)
                link(nc.vector.tensor_tensor(ys, ys, over_c(dout[:, p * HT:(p + 1) * HT]), ALU.mult))
                link(nc.vector.tensor_tensor(xs, yps[:, :], xs, ALU.add))
                centre(b, 2 + p, xs, hs)

            def first_relu(b, p):
                hs = half(h1, p)
                dve.wait_ge(rstd_made, NORMS * b + 3 + p)
                nc.vector.scalar_tensor_tensor(out=tiles(hs), in0=tiles(hs), scalar=0.0,
                                               in1=over_c(rstd[:, p, :]), op0=ALU.max, op1=ALU.mult).then_inc(h_made, 1)

            def layer_residual(b, l, p):
                src, dst = half(reads[l], p), half(writes[l], p)
                dve.wait_ge(y_done, OUTS * b + 3 + 2 * l + p)
                link(nc.vector.tensor_tensor(dst, yps[:, :], src, ALU.add))
                link(nc.vector.tensor_tensor(tiles(dst), tiles(dst), over_t(bs[:, l, :]), ALU.add))
                centre(b, 4 + 2 * l + p, dst, dst)

            def layer_relu(b, l, p):
                dst = half(writes[l], p)
                dve.wait_ge(rstd_made, NORMS * b + 5 + 2 * l + p)
                link(nc.vector.tensor_tensor(tiles(dst), tiles(dst), over_c(rstd[:, p, :]), ALU.mult))
                link(nc.vector.tensor_tensor(tiles(dst), tiles(dst), over_t(gs[:, l, :]), ALU.mult))
                link(nc.vector.tensor_tensor(tiles(dst), tiles(dst), over_t(be[:, l, :]), ALU.add))
                if l < L - 1:
                    nc.vector.tensor_scalar(dst, dst, 0.0, None, ALU.max).then_inc(h_made, 1)
                else:
                    nc.vector.scalar_tensor_tensor(out=dst, in0=dst, scalar=0.0, in1=half(xr, p),
                                                   op0=ALU.max, op1=ALU.add).then_inc(result, 1)

            def norms_to_layers(b):
                for p in range(2):
                    first_residual(b, p)
                    variance(b, 2 + p)
                    first_relu(b, p)
                for l in range(L - 1):
                    for p in range(2):
                        layer_residual(b, l, p)
                        variance(b, 4 + 2 * l + p)
                        layer_relu(b, l, p)

            dve.wait_ge(u_loaded, 16)
            parts_l = (0, 0, 1, 1, 0, 2, 1, 2)
            parts_r = (0, 1, 0, 1, 2, 0, 2, 1)
            nc.vector.memset(expo[:, :], -0.5)
            nc.vector.memset(rows[:, :, :], 0.0)
            nc.vector.memset(ones[:, :], 1.0).then_inc(ones_made, 1)
            rest = u_in
            for m in range(3):
                link(nc.vector.tensor_copy(u_part[m], rest))
                if m < 2:
                    link(nc.vector.tensor_tensor(u_rest[m], rest, u_part[m], ALU.subtract))
                    rest = u_rest[m]
            for side, parts in enumerate((parts_l, parts_r)):
                for q, m in enumerate(parts):
                    i = nc.vector.tensor_copy(cat[side][:, :, q * R:(q + 1) * R], u_part[m])
                i.then_inc(u_split, 1)
            for side, dst in enumerate((ul, ur)):
                for q in range(NC):
                    dve.wait_ge(u_turned, side * NC + q + 1)
                    nc.vector.tensor_copy(dst[:, q * CH:(q + 1) * CH], ring[:, q, :]).then_inc(u_ready, 1)
            dve.wait_ge(const_in, 16 * 6)
            for u in range(NB + 1):
                if u < NB:
                    add_transposed(0, u)
                if u >= 1:
                    times_gate(0, u - 1)
                if u in (3, 5):
                    first_norm(0, (u - 3) // 2)
                if u in (6, 8):
                    variance(0, (u - 6) // 2)
            degrees(0)
            before = steps[0]

            with dve.Fori(0, B - 1) as b:
                steps_before[0] = STEPS_BATCH * b
                norms_to_layers(b)
                for u in range(NB + 1):
                    if u < NB:
                        add_transposed(b + 1, u)
                    if u >= 1:
                        times_gate(b + 1, u - 1)
                    at = BUILD[u] if u < NB else None
                    if at == (10, 0):
                        layer_residual(b, L - 1, 0)
                    if at == (10, 2):
                        variance(b, 2 + 2 * L)
                    if at == (11, 1):
                        layer_relu(b, L - 1, 0)
                    if at == (12, 0):
                        layer_residual(b, L - 1, 1)
                    if at == (12, 2):
                        variance(b, 3 + 2 * L)
                    if at == (13, 0):
                        layer_relu(b, L - 1, 1)
                for p in range(2):
                    first_norm(b + 1, p)
                    variance(b + 1, p)
                degrees(b + 1)
                assert steps[0] - before == STEPS_BATCH, (steps[0] - before)
            steps_before[0] = STEPS_BATCH * (B - 2)
            norms_to_layers(B - 1)
            for p in range(2):
                layer_residual(B - 1, L - 1, p)
                variance(B - 1, 2 + 2 * L + p)
                layer_relu(B - 1, L - 1, p)


_INS = ["x", "adj", "L0_gnn_U", "L0_gnn_w_scale", "L1_gnn_W", "L1_gnn_b", "L1_gnn_gamma", "L1_gnn_beta"]


def kernel(**inputs):
    import numpy as _np
    import concourse.bacc as _bacc
    from concourse import mybir as _mybir
    from concourse.bass_utils import run_bass_kernel_spmd as _run

    nc = _bacc.Bacc("TRN2", target_bir_lowering=False, num_devices=1, dynamic_dma_scratch_size=512)
    arrays, args = {}, []
    for name in _INS:
        a = _np.ascontiguousarray(inputs[name])
        if a.ndim == 0:
            a = a.reshape(1)
        arrays[f"in_{name}_dram"] = a
        args.append(nc.dram_tensor(f"in_{name}_dram", a.shape, _mybir.dt.from_np(a.dtype), kind="ExternalInput").ap())
    shape = inputs["x"].shape
    args.append(nc.dram_tensor("out_dram", shape, _mybir.dt.float32, kind="ExternalOutput").ap())
    adjacency_mixer_kernel(nc, *args)
    r = _run(nc, [arrays], core_ids=[0])
    return r.results[0]["out_dram"]
```

```python
import concourse.bass as bass
from concourse import mybir
from contextlib import ExitStack


def adjacency_mixer_kernel(nc, x, adj, U, w_scale, W, bias, gamma, beta, out):
    fp32 = mybir.dt.float32
    bf16 = mybir.dt.bfloat16
    ALU = mybir.AluOpType
    ACT = mybir.ActivationFunctionType
    AX = mybir.AxisListType

    B, N, C = x.shape
    R = U.shape[1]
    L = W.shape[0]
    P = 128
    T = N // P
    CH = 512
    NC = N // CH
    TC = CH // P
    HT = T // 2
    HC = HT * C
    DEG_EPS = 1e-12
    LN_EPS = 1e-5

    BUILD = [(j, c) for j in range(T) for c in range(j // TC + 1)]
    NB = len(BUILD)
    AFFINE = 4
    OUTS = 2 + 2 * L

    def build_cols(j, c):
        return min((c + 1) * TC, j + 1) * P - c * CH

    def strip(j):
        return j * (j + 1) // 2 * P

    def flipped(i, c):
        return list(range(max(TC * c, i + 1), TC * (c + 1)))

    FLIPS = [[(half, i, 2 * half + odd) for half in range(2) for i in range(T) if flipped(i, 2 * half + odd)]
             for odd in range(2)]
    NF = [len(f) for f in FLIPS]
    NF0 = [sum(half == 0 for half, _, _ in f) for f in FLIPS]
    TURNS = [min(2 * T, max(8 + 2 * min(u, TC) + max(u - TC, 0), 0)) for u in range(NB + 1)]
    LAST_LEAVES = (TURNS.index(2 * T) + 3, TURNS.index(2 * T) + 8)
    LAST_NORMS = [u + 1 for u in LAST_LEAVES]
    RING = 4

    ctx = ExitStack()
    with ctx:
        def sb(name, shape, dt=fp32):
            return ctx.enter_context(nc.sbuf_tensor(name, shape, dt))

        def sem(name):
            return ctx.enter_context(nc.semaphore(name))

        Wt = sb("adjacency", [P, T, N])
        Kt = sb("k_lower", [P, strip(T)])
        ul = sb("u_left", [P, N], bf16)
        ur = sb("u_right", [P, N], bf16)
        xr = sb("x_residual", [P, T * C])
        hA = sb("h_a", [P, T * C])
        hB = sb("h_b", [P, T * C])
        G = sb("product_out", [P, CH])
        ident = sb("ident", [P, P])
        wl = sb("weights_twice", [P, L, 2 * C])
        bs = sb("bias_rows", [P, L, C])
        gs = sb("gamma_rows", [P, L, C])
        be = sb("beta_rows", [P, L, C])
        ws = sb("w_scale_col", [P, 1])
        ones = sb("ones", [P, 32])
        expo = sb("minus_half", [P, T])
        rows = sb("row_sums", [P, T, NC])
        deg = sb("degree", [P, T])
        dis = sb("degree_rsqrt", [P, T])
        dout = sb("degree_out", [P, T])
        rd = sb("norm_times_degree", [P, T])
        mean = sb("mean", [P, HT])
        var = sb("variance", [P, 2, HT])
        rstd = sb("rstd", [P, 2, HT])
        x_var = sb("x_variance", [P, T])
        x_rstd = sb("x_rstd", [P, T])

        KIND = 8
        cat = [Kt[:, m * T * P:(m + 1) * T * P].rearrange("p (t k) -> p t k", t=T) for m in range(2)]
        u_in = hA[:, 0:T * R].rearrange("p (t r) -> p t r", t=T)
        u_rest = [hA[:, (1 + m) * T * R:(2 + m) * T * R].rearrange("p (t r) -> p t r", t=T) for m in range(2)]
        u_part = [hB[:, m * T * R // 2:(m + 1) * T * R // 2].bitcast(bf16).rearrange("p (t r) -> p t r", t=T)
                  for m in range(3)]

        x_new = Kt[:, strip(T) - T * C:strip(T)]
        h1 = Kt[:, 0:T * C]
        turned_sb = hA[:, :].rearrange("p (s n) -> p s n", s=2)

        acc = ctx.enter_context(nc.psum_tensor("acc", [P, 2, CH], fp32))
        ring = ctx.enter_context(nc.psum_tensor("ring", [P, RING, CH], fp32))
        col = ctx.enter_context(nc.psum_tensor("column_sums", [P, CH], fp32))
        yps = ctx.enter_context(nc.psum_tensor("y_psum", [P, CH], fp32))

        w_in = [sem(f"strip_in_{j}") for j in range(T)]
        u_loaded = sem("u_loaded")
        const_in = sem("const_in")
        x_in = sem("x_in")
        xr_in = sem("xr_in")
        out_stored = sem("out_stored")
        wl_zeroed = sem("wl_zeroed")
        ident_made = sem("ident_made")
        ones_made = sem("ones_made")
        u_split = sem("u_split")
        u_turned = sem("u_turned")
        u_ready = sem("u_ready")
        gate_in = sem("gate_in")
        gated = sem("gated")
        turned_in = sem("turned_in")
        summed = sem("summed")
        k_made = sem("k_made")
        cols_summed = sem("cols_summed")
        cols_out = sem("cols_out")
        cols_turned = sem("cols_turned")
        deg_made = sem("deg_made")
        dis_made = sem("dis_made")
        dh_made = sem("dh_made")
        flip_in = [sem(f"flip_in_{side}") for side in ("even", "odd")]
        flip_out = [sem(f"flip_out_{side}") for side in ("even", "odd")]
        flip_used = [sem(f"flip_used_{side}") for side in ("even", "odd")]
        acc_done = sem("acc_done")
        g_out = sem("g_out")
        y_done = sem("y_done")
        x_centred = sem("x_centred")
        x_squared = sem("x_squared")
        x_var_made = sem("x_var_made")
        x_rstd_made = sem("x_rstd_made")
        x_moved = sem("x_moved")
        centred = sem("centred")
        squared = sem("squared")
        var_made = sem("var_made")
        rstd_made = sem("rstd_made")
        h_made = sem("h_made")
        strip_free = sem("strip_free")
        affine = sem("affine_step")
        affined = sem("affined")
        result = sem("result")
        step = sem("vector_step")

        def half(ap, p):
            return ap[:, p * HC:(p + 1) * HC]

        def tiles(ap):
            return ap.rearrange("p (t c) -> p t c", c=C)

        def over_c(ap):
            return ap.unsqueeze(2).broadcast_to([P, HT, C])

        def over_t(ap):
            return ap.unsqueeze(1).broadcast_to([P, HT, C])

        reads = [h1, hA[:, :], hB[:, :]]
        writes = [hA[:, :], hB[:, :], hA[:, :]]

        block = ctx.enter_context(nc.Block())

        @block.sync
        def _(sp):
            def load_x(b, dst, loaded):
                sp.dma_start(tiles(dst), x[b].rearrange("(t p) c -> p t c", p=P)).then_inc(loaded, 16)

            def load_strip(b, j):
                sp.dma_start(Wt[:, j, :], adj[b, j * P:(j + 1) * P, :]).then_inc(w_in[j], 16)

            sp.dma_start(u_in, U.rearrange("(t p) r -> p t r", p=P)).then_inc(u_loaded, 16)
            load_x(0, x_new, x_in)
            load_strip(0, 0)
            for q in range(2):
                sp.wait_ge(wl_zeroed, 1)
                sp.dma_start(wl[q * C:(q + 1) * C, :, q * C:(q + 1) * C], W.rearrange("l d e -> d l e")).then_inc(const_in, 16)
            for rows_sb, src in ((bs, bias), (gs, gamma), (be, beta)):
                sp.dma_start(rows_sb[:, :, :], src.partition_broadcast(P)).then_inc(const_in, 16)
            sp.dma_start(ws[:, :], w_scale.partition_broadcast(P)).then_inc(const_in, 16)
            load_x(0, xr[:, :], xr_in)
            for j in range(1, T):
                load_strip(0, j)

            def store(b):
                sp.wait_ge(result, 2 * b + 2)
                sp.dma_start(out[b].rearrange("(t p) c -> p t c", p=P), tiles(hA[:, :])).then_inc(out_stored, 16)

            with sp.Fori(0, B - 1) as b:
                sp.wait_ge(centred, OUTS * b + 2)
                load_x(b + 1, x_new, x_in)
                for j in range(T):
                    if j < T - 1:
                        sp.wait_ge(strip_free, (T - 1) * b + j + 1)
                    else:
                        sp.wait_ge(acc_done, OUTS * (b + 1))
                    load_strip(b + 1, j)
                store(b)
                sp.wait_ge(out_stored, 16 * (b + 1))
                load_x(b + 1, xr[:, :], xr_in)
            store(B - 1)
            sp.wait_ge(out_stored, 16 * B)

        @block.tensor
        def _(pe):
            def product(bank, h, j, c):
                o = C * (c % 2)
                return nc.tensor.matmul(acc[o:o + C, bank, :], h[:, j * C:(j + 1) * C],
                                        Wt[:, j, c * CH:(c + 1) * CH], start=(j == 0), stop=(j == T - 1))

            def layer_step(b, l, j, halves=(0, 1)):
                for p in halves:
                    if j == 0:
                        pe.wait_ge(g_out, OUTS * b + 2 * l + p + 1)
                    if j % HT == 0:
                        pe.wait_ge(h_made, 2 * L * b + 2 * l + j // HT + 1)
                    for c in (2 * p, 2 * p + 1):
                        m = product(p, reads[l], j, c)
                    if j == T - 1:
                        m.then_inc(acc_done, 1)
                return m

            def leave(b, n):
                pe.wait_ge(g_out, OUTS * b + n + 1)
                if n == 0:
                    pe.wait_ge(deg_made, b + 1)
                else:
                    pe.wait_ge(var_made, OUTS * b + n)
                rhs = ident[:, :] if n < 2 else wl[:, (n - 2) // 2, :]
                by_chunk = yps[:, :].rearrange("p (a k c) -> p a k c", a=2, c=C)
                for k in range(TC):
                    m = nc.tensor.matmul(by_chunk[:, :, k, :], G[:, k * P:(k + 1) * P], rhs, start=True, stop=True)
                m.then_inc(y_done, 1)

            def build_transposes(b, u):
                j, c = BUILD[u]
                if c == 0:
                    pe.wait_ge(w_in[j], 16 * (b + 1))
                if u == 0:
                    pe.wait_ge(x_var_made, 2 * b + 2)
                if u >= 2 or not isinstance(b, int):
                    pe.wait_ge(summed, NB * b + u - 1)
                for k in range(build_cols(j, c) // P):
                    m = nc.tensor.transpose(ring[:, 2 + u % 2, k * P:(k + 1) * P],
                                            Wt[:, c * TC + k, j * P:(j + 1) * P], ident[:, :])
                m.then_inc(turned_in, 1)

            def build_gate(b, u):
                j, c = BUILD[u]
                n = build_cols(j, c)
                if u >= 2 or not isinstance(b, int):
                    pe.wait_ge(k_made, NB * b + u - 1)
                nc.tensor.matmul(ring[:, u % 2, 0:n], ul[:, j * P:(j + 1) * P], ur[:, c * CH:c * CH + n],
                                 start=True, stop=True).then_inc(gate_in, 1)

            def column_sums(b, j):
                pe.wait_ge(k_made, NB * b + BUILD.index((j, j // TC)) + 1)
                for c in range((j - 1) // TC + 1):
                    n = min(CH, (j - c * TC) * P)
                    m = nc.tensor.matmul(col[32 * c:32 * c + 32, 0:n], ones[:, :],
                                         Kt[:, strip(j) + c * CH:strip(j) + c * CH + n],
                                         start=(j == c * TC + 1), stop=(j == T - 1), skip_group_check=True)
                if j == T - 1:
                    m.then_inc(cols_summed, 1)

            def column_sums_after(b, u):
                if u >= 0:
                    j, c = BUILD[u]
                    if 0 < j < T - 1 and c == j // TC:
                        column_sums(b, j)

            def build_tail(b):
                column_sums(b, T - 1)
                pe.wait_ge(cols_out, 2 * b + 2)
                if not isinstance(b, int):
                    pe.wait_ge(var_made, OUTS * b)
                by_chunk = yps[:, 0:T].rearrange("p (c k) -> p c k", k=TC)
                for k in range(TC):
                    n = NC if k < TC - 1 else NC - 1
                    m = nc.tensor.matmul(by_chunk[:, 0:n, k], G[0:32 * n, k * P:(k + 1) * P],
                                         ident[0:32 * n, 0:32 * (n - 1) + 1:32], start=True, stop=True)
                m.then_inc(cols_turned, 1)

            def flip(b, p, i):
                for odd in range(2):
                    c = 2 * p + odd
                    if (p, i, c) not in FLIPS[odd]:
                        continue
                    v = FLIPS[odd].index((p, i, c))
                    if v == 0:
                        pe.wait_ge(k_made, NB * (b + 1))
                    if v >= 2:
                        pe.wait_ge(flip_out[odd], NF[odd] * b + v - 1)
                    for k, j in enumerate(flipped(i, c)):
                        m = nc.tensor.transpose(ring[:, 2 * odd + v % 2, k * P:(k + 1) * P],
                                                Kt[:, strip(j) + i * P:strip(j) + (i + 1) * P], ident[:, :])
                    m.then_inc(flip_in[odd], 1)

            def k_product(b):
                flip(b, 0, 0)
                for p in range(2):
                    for i in range(T):
                        if p == 0 and i % HT == 0:
                            pe.wait_ge(dh_made, 2 * b + i // HT + 1)
                        if i + 1 < T:
                            flip(b, p, i + 1)
                        elif p == 0:
                            flip(b, 1, 0)
                        dh = hB[:, i * C:(i + 1) * C]
                        for odd in range(2):
                            c, o = 2 * p + odd, C * odd
                            if TC * c <= i:
                                n = min(CH, (i + 1) * P - c * CH)
                                m = nc.tensor.matmul(acc[o:o + C, p, 0:n], dh,
                                                     Kt[:, strip(i) + c * CH:strip(i) + c * CH + n],
                                                     start=(i == 0), stop=(i == T - 1), skip_group_check=True)
                        if i == T - 1:
                            m.then_inc(acc_done, 1)
                        for odd in range(2):
                            c, o = 2 * p + odd, C * odd
                            if (p, i, c) in FLIPS[odd]:
                                v = FLIPS[odd].index((p, i, c))
                                lo = flipped(i, c)[0] * P - c * CH
                                pe.wait_ge(flip_out[odd], NF[odd] * b + v + 1)
                                nc.tensor.matmul(acc[o:o + C, p, lo:CH], dh, turned_sb[:, odd, 0:CH - lo],
                                                 start=(i == 0 and c > 0), stop=False, skip_group_check=True)\
                                  .then_inc(flip_used[odd], 1)
                        if p == 1 and i == 2:
                            leave(b, 0)

            def full_layer(b, l):
                for p, steps in ((0, range(0, 8)), (1, range(0, 4)), (0, range(8, 16)), (1, range(4, 16))):
                    for j in steps:
                        layer_step(b, l, j, (p,))
                        if (p, j) == (0, 2):
                            leave(b, 2 * l + 1)
                        if (p, j) == (1, 6):
                            leave(b, 2 * l + 2)

            def last_layer_turn(b, k):
                j, p = k // 2, k % 2
                if j < 3:
                    j, p = k % 3, k // 3
                if k == 3:
                    leave(b, 2 * L - 1)
                m = layer_step(b, L - 1, j, (p,))
                if p == 1 and j < T - 1:
                    m.then_inc(strip_free, 1)

            def window(b):
                turn = 0
                for u in range(NB + 1):
                    turns = TURNS[u]
                    while turn < turns - 1:
                        last_layer_turn(b, turn)
                        turn += 1
                    if u < NB:
                        build_transposes(b + 1, u)
                    while turn < turns:
                        last_layer_turn(b, turn)
                        turn += 1
                    if u > 0:
                        build_gate(b + 1, u - 1)
                        column_sums_after(b + 1, u - 3)
                    for p in range(2):
                        if u == LAST_LEAVES[p]:
                            leave(b, 2 * L + p)
                column_sums_after(b + 1, NB - 2)
                build_tail(b + 1)

            pe.wait_ge(ident_made, 2)
            for m in range(2):
                pe.wait_ge(u_split, m + 1)
                for q in range(NC):
                    if m == 1:
                        pe.wait_ge(u_ready, q + 1)
                    for k in range(TC):
                        t = nc.tensor.transpose(ring[:, q, k * P:(k + 1) * P], cat[m][:, q * TC + k, :], ident[:, :])
                    t.then_inc(u_turned, 1)
            pe.wait_ge(u_ready, 2 * NC)
            pe.wait_ge(ones_made, 1)
            for u in range(NB + 1):
                if u < NB:
                    build_transposes(0, u)
                if u > 0:
                    build_gate(0, u - 1)
                    column_sums_after(0, u - 3)
            column_sums_after(0, NB - 2)
            build_tail(0)

            with pe.Fori(0, B - 1) as b:
                k_product(b)
                for l in range(L - 1):
                    full_layer(b, l)
                window(b)
            k_product(B - 1)
            for l in range(L - 1):
                full_layer(B - 1, l)
            for k in range(2 * T):
                last_layer_turn(B - 1, k)
            leave(B - 1, 2 * L)
            leave(B - 1, 2 * L + 1)

        @block.scalar
        def _(act):
            def gate(b, u):
                j, c = BUILD[u]
                n = build_cols(j, c)
                act.wait_ge(gate_in, NB * b + u + 1)
                nc.scalar.activation(ring[:, u % 2, 0:n], ring[:, u % 2, 0:n], ACT.Sigmoid).then_inc(gated, 1)

            def square(b, n, src):
                act.wait_ge(centred, OUTS * b + n + 1)
                if n > 0:
                    act.wait_ge(var_made, OUTS * b + n)
                nc.scalar.activation(yps[:, :], src, ACT.Square).then_inc(squared, 1)

            def square_x(b, p):
                act.wait_ge(x_centred, 2 * b + p + 1)
                nc.scalar.activation(ring[:, 2 + p, :], half(x_new, p), ACT.Square).then_inc(x_squared, 1)

            def move_x(b):
                act.wait_ge(x_centred, 2 * b + 2)
                if not isinstance(b, int):
                    act.wait_ge(centred, OUTS * b)
                for p in range(2):
                    nc.scalar.activation(half(hB, p), half(x_new, p), ACT.Relu).then_inc(x_moved, 1)

            def product_out(b, n):
                act.wait_ge(acc_done, OUTS * b + n + 1)
                if n == 0:
                    act.wait_ge(cols_turned, b + 1)
                else:
                    act.wait_ge(y_done, OUTS * b + n)
                nc.scalar.activation(G[:, :], acc[:, n % 2, :], ACT.Copy).then_inc(g_out, 1)

            def cols_to_sbuf(b):
                act.wait_ge(cols_summed, b + 1)
                if not isinstance(b, int):
                    act.wait_ge(y_done, OUTS * b)
                nc.scalar.activation(G[0:96, :], col[0:96, :], ACT.Copy).then_inc(cols_out, 1)
                nc.scalar.activation(G[96:128, 0:CH - P], col[96:128, 0:CH - P], ACT.Copy).then_inc(cols_out, 1)

            def flip_to_sbuf(b, v):
                _, i, c = FLIPS[0][v]
                n = len(flipped(i, c)) * P
                act.wait_ge(flip_in[0], NF[0] * b + v + 1)
                if v > 0:
                    act.wait_ge(flip_used[0], NF[0] * b + v)
                else:
                    act.wait_ge(xr_in, 16 * (b + 1))
                nc.scalar.activation(turned_sb[:, 0, 0:n], ring[:, v % 2, 0:n], ACT.Copy).then_inc(flip_out[0], 1)

            def k_and_layers(b):
                for v in range(NF[0]):
                    flip_to_sbuf(b, v)
                    if v == NF0[0]:
                        product_out(b, 0)
                    if v == NF0[0] + 6:
                        square(b, 0, half(h1, 0))
                product_out(b, 1)
                square(b, 1, half(h1, 1))
                for l in range(L - 1):
                    for p in range(2):
                        product_out(b, 2 + 2 * l + p)
                        square(b, 2 + 2 * l + p, half(writes[l], p))
                        if (l, p) == (0, 1) and not isinstance(b, int):
                            square_x(b + 1, 0)
                            square_x(b + 1, 1)

            def last_out(b, p):
                product_out(b, 2 * L + p)
                square(b, 2 * L + p, half(writes[L - 1], p))

            square_x(0, 0)
            square_x(0, 1)
            for u in range(NB):
                gate(0, u)
                if u == 4:
                    move_x(0)
            cols_to_sbuf(0)
            with act.Fori(0, B - 1) as b:
                k_and_layers(b)
                for u in range(NB):
                    gate(b + 1, u)
                    for p in range(2):
                        if u == LAST_LEAVES[p] - 2:
                            product_out(b, 2 * L + p)
                        if u == LAST_NORMS[p]:
                            square(b, 2 * L + p, half(writes[L - 1], p))
                    if u == LAST_NORMS[1] + 2:
                        move_x(b + 1)
                cols_to_sbuf(b + 1)
            k_and_layers(B - 1)
            last_out(B - 1, 0)
            last_out(B - 1, 1)

        @block.gpsimd
        def _(pool):
            pool.memset(wl[:, :, :], 0.0).then_inc(wl_zeroed, 1)
            pool.memset(ident[:, :], 0.0).then_inc(ident_made, 1)
            pool.wait_ge(ident_made, 1)
            pool.affine_select(out=ident[:, :], in_=ident[:, :], compare_op=ALU.not_equal, fill=1.0,
                               base=0, pattern=[[-1, P]], channel_multiplier=1).then_inc(ident_made, 1)
            pool.wait_ge(ones_made, 1)

            def root(b, n):
                pool.wait_ge(var_made, OUTS * b + n + 1)
                nc.gpsimd.tensor_tensor(rstd[:, n % 2, :], var[:, n % 2, :], expo[:, 0:HT], ALU.pow).then_inc(rstd_made, 1)

            def degree_root(b, p):
                pool.wait_ge(deg_made, b + 1)
                mine = slice(p * HT, (p + 1) * HT)
                nc.gpsimd.tensor_tensor(dis[:, mine], deg[:, mine], expo[:, 0:HT], ALU.pow).then_inc(dis_made, 1)

            def last_affine(b, p):
                dst = half(writes[L - 1], p)
                pool.wait_ge(rstd_made, OUTS * b + 1 + 2 * L + p)
                a = AFFINE * b + 2 * p
                nc.gpsimd.tensor_tensor(tiles(dst), tiles(dst), over_c(rstd[:, p, :]), ALU.mult).then_inc(affine, 1)
                pool.wait_ge(affine, a + 1)
                nc.gpsimd.tensor_tensor(tiles(dst), tiles(dst), over_t(gs[:, L - 1, :]), ALU.mult).then_inc(affine, 1)
                pool.wait_ge(affine, a + 2)
                nc.gpsimd.tensor_tensor(tiles(dst), tiles(dst), over_t(be[:, L - 1, :]), ALU.add).then_inc(affined, 1)

            def x_root(b):
                for p in range(2):
                    mine = slice(p * HT, (p + 1) * HT)
                    pool.wait_ge(x_var_made, 2 * b + p + 1)
                    nc.gpsimd.tensor_tensor(x_rstd[:, mine], x_var[:, mine], expo[:, 0:HT], ALU.pow)\
                      .then_inc(x_rstd_made, 1)

            def norm_roots(b):
                for p in range(2):
                    degree_root(b, p)
                for n in range(OUTS):
                    root(b, n)
                    if n == 3 and not isinstance(b, int):
                        x_root(b + 1)
                    if n >= 2 * L:
                        last_affine(b, n - 2 * L)

            x_root(0)
            with pool.Fori(0, B - 1) as b:
                norm_roots(b)
            norm_roots(B - 1)

        STEPS_BATCH = 3 * (OUTS + 2) + 5 + 2 * 2 + 2 * L * 5 - 2 * 3

        @block.vector
        def _(dve):
            steps = [0]
            steps_before = [0]

            def link(instruction):
                steps[0] += 1
                instruction.then_inc(step, 1)
                dve.wait_ge(step, steps[0] + steps_before[0])

            def add_transposed(b, u):
                j, c = BUILD[u]
                n = build_cols(j, c)
                at = strip(j) + c * CH
                dve.wait_ge(w_in[j], 16 * (b + 1))
                dve.wait_ge(turned_in, NB * b + u + 1)
                if (j, c) == (T - 1, NC // 2):
                    dve.wait_ge(x_moved, 2 * b + 2)
                nc.vector.tensor_tensor(Kt[:, at:at + n], Wt[:, j, c * CH:c * CH + n], ring[:, 2 + u % 2, 0:n],
                                        ALU.add).then_inc(summed, 1)

            def times_gate(b, u):
                j, c = BUILD[u]
                n = build_cols(j, c)
                at = strip(j) + c * CH
                dve.wait_ge(summed, NB * b + u + 1)
                dve.wait_ge(gated, NB * b + u + 1)
                nc.vector.scalar_tensor_tensor(out=Kt[:, at:at + n], in0=Kt[:, at:at + n], scalar=1.0,
                                               in1=ring[:, u % 2, 0:n], op0=ALU.mult, op1=ALU.mult,
                                               accum_out=rows[:, j, c:c + 1]).then_inc(k_made, 1)

            def centre(src, dst, done):
                link(nc.vector.tensor_reduce(mean[:, :], tiles(src), AX.X, ALU.add))
                link(nc.vector.tensor_scalar(mean[:, :], mean[:, :], 1.0 / C, None, ALU.mult))
                nc.vector.tensor_tensor(tiles(dst), tiles(src), over_c(mean[:, :]), ALU.subtract).then_inc(done, 1)

            def variance(b, n):
                dve.wait_ge(squared, OUTS * b + n + 1)
                link(nc.vector.tensor_reduce(var[:, n % 2, :], tiles(yps[:, :]), AX.X, ALU.add))
                nc.vector.tensor_scalar(var[:, n % 2, :], var[:, n % 2, :], 1.0 / C, LN_EPS, ALU.mult, ALU.add)\
                  .then_inc(var_made, 1)

            def x_norm(b):
                dve.wait_ge(x_in, 16 * (b + 1))
                for p in range(2):
                    if p > 0:
                        dve.wait_ge(x_centred, 2 * b + 1)
                    centre(half(x_new, p), half(x_new, p), x_centred)
                for p in range(2):
                    mine = slice(p * HT, (p + 1) * HT)
                    dve.wait_ge(x_squared, 2 * b + p + 1)
                    link(nc.vector.tensor_reduce(x_var[:, mine], tiles(ring[:, 2 + p, :]), AX.X, ALU.add))
                    nc.vector.tensor_scalar(x_var[:, mine], x_var[:, mine], 1.0 / C, LN_EPS, ALU.mult, ALU.add)\
                      .then_inc(x_var_made, 1)

            def degrees(b):
                dve.wait_ge(k_made, NB * (b + 1))
                link(nc.vector.tensor_reduce(deg[:, :], rows[:, :, :], AX.X, ALU.add))
                dve.wait_ge(cols_turned, b + 1)
                link(nc.vector.tensor_tensor(deg[:, 0:T - 1], deg[:, 0:T - 1], yps[:, 0:T - 1], ALU.add))
                nc.vector.tensor_scalar(deg[:, :], deg[:, :], 0.5, DEG_EPS, ALU.mult, ALU.max).then_inc(deg_made, 1)
                dve.wait_ge(x_rstd_made, 2 * b + 2)
                dve.wait_ge(x_moved, 2 * b + 2)
                for p in range(2):
                    dve.wait_ge(dis_made, 2 * b + p + 1)
                    mine = slice(p * HT, (p + 1) * HT)
                    link(nc.vector.tensor_tensor(rd[:, mine], dis[:, mine], x_rstd[:, mine], ALU.mult))
                    h = tiles(half(hB, p))
                    nc.vector.tensor_tensor(h, h, over_c(rd[:, mine]), ALU.mult).then_inc(dh_made, 1)
                link(nc.vector.tensor_scalar(dout[:, :], dis[:, :], ws[:, 0:1], 0.5, ALU.mult, ALU.mult))

            def flip_to_sbuf(b, v):
                _, i, c = FLIPS[1][v]
                n = len(flipped(i, c)) * P
                dve.wait_ge(flip_in[1], NF[1] * b + v + 1)
                if v > 0:
                    dve.wait_ge(flip_used[1], NF[1] * b + v)
                else:
                    dve.wait_ge(xr_in, 16 * (b + 1))
                nc.vector.tensor_copy(turned_sb[:, 1, 0:n], ring[:, 2 + v % 2, 0:n]).then_inc(flip_out[1], 1)

            def first_residual(b, p):
                dve.wait_ge(y_done, OUTS * b + p + 1)
                ys, xs, hs = tiles(yps[:, :]), half(xr, p), half(h1, p)
                link(nc.vector.tensor_tensor(ys, ys, over_c(dout[:, p * HT:(p + 1) * HT]), ALU.mult))
                dve.wait_ge(xr_in, 16 * (b + 1))
                link(nc.vector.tensor_tensor(xs, yps[:, :], xs, ALU.add))
                centre(xs, hs, centred)

            def first_relu(b, p):
                hs = half(h1, p)
                dve.wait_ge(rstd_made, OUTS * b + 1 + p)
                nc.vector.scalar_tensor_tensor(out=tiles(hs), in0=tiles(hs), scalar=0.0,
                                               in1=over_c(rstd[:, p, :]), op0=ALU.max, op1=ALU.mult).then_inc(h_made, 1)

            def layer_residual(b, l, p):
                src, dst = half(reads[l], p), half(writes[l], p)
                dve.wait_ge(y_done, OUTS * b + 3 + 2 * l + p)
                link(nc.vector.tensor_tensor(dst, yps[:, :], src, ALU.add))
                link(nc.vector.tensor_tensor(tiles(dst), tiles(dst), over_t(bs[:, l, :]), ALU.add))
                centre(dst, dst, centred)

            def layer_relu(b, l, p):
                dst = half(writes[l], p)
                dve.wait_ge(rstd_made, OUTS * b + 3 + 2 * l + p)
                link(nc.vector.tensor_tensor(tiles(dst), tiles(dst), over_c(rstd[:, p, :]), ALU.mult))
                link(nc.vector.tensor_tensor(tiles(dst), tiles(dst), over_t(gs[:, l, :]), ALU.mult))
                link(nc.vector.tensor_tensor(tiles(dst), tiles(dst), over_t(be[:, l, :]), ALU.add))
                nc.vector.tensor_scalar(dst, dst, 0.0, None, ALU.max).then_inc(h_made, 1)

            def last_relu(b, p):
                dst = half(writes[L - 1], p)
                dve.wait_ge(affined, 2 * b + p + 1)
                nc.vector.scalar_tensor_tensor(out=dst, in0=dst, scalar=0.0, in1=half(xr, p),
                                               op0=ALU.max, op1=ALU.add).then_inc(result, 1)

            def norms_to_layers(b):
                for v in range(NF[1]):
                    flip_to_sbuf(b, v)
                    if v == NF0[1] + 4:
                        first_residual(b, 0)
                    if v == NF0[1] + 6:
                        variance(b, 0)
                    if v == NF0[1] + 7:
                        first_relu(b, 0)
                first_residual(b, 1)
                variance(b, 1)
                first_relu(b, 1)
                for l in range(L - 1):
                    for p in range(2):
                        layer_residual(b, l, p)
                        variance(b, 2 + 2 * l + p)
                        layer_relu(b, l, p)
                        if (l, p) == (0, 1) and not isinstance(b, int):
                            x_norm(b + 1)

            dve.wait_ge(u_loaded, 16)
            parts_l = (0, 0, 1, 1, 0, 2, 1, 2)
            parts_r = (0, 1, 0, 1, 2, 0, 2, 1)
            nc.vector.memset(expo[:, :], -0.5)
            nc.vector.memset(rows[:, :, :], 0.0)
            nc.vector.memset(ones[:, :], 1.0).then_inc(ones_made, 1)
            rest = u_in
            for m in range(3):
                link(nc.vector.tensor_copy(u_part[m], rest))
                if m < 2:
                    link(nc.vector.tensor_tensor(u_rest[m], rest, u_part[m], ALU.subtract))
                    rest = u_rest[m]
            for side, parts in enumerate((parts_l, parts_r)):
                for q, m in enumerate(parts):
                    i = nc.vector.tensor_copy(cat[side][:, :, q * R:(q + 1) * R], u_part[m])
                i.then_inc(u_split, 1)
            for side, dst in enumerate((ul, ur)):
                for q in range(NC):
                    dve.wait_ge(u_turned, side * NC + q + 1)
                    nc.vector.tensor_copy(dst[:, q * CH:(q + 1) * CH], ring[:, q, :]).then_inc(u_ready, 1)
            dve.wait_ge(const_in, 16 * 6)
            x_norm(0)
            for u in range(NB + 1):
                if u < NB:
                    add_transposed(0, u)
                if u >= 1:
                    times_gate(0, u - 1)
            degrees(0)
            before = steps[0]

            with dve.Fori(0, B - 1) as b:
                steps_before[0] = STEPS_BATCH * b
                norms_to_layers(b)
                for u in range(NB + 1):
                    if u < NB:
                        add_transposed(b + 1, u)
                    if u >= 1:
                        times_gate(b + 1, u - 1)
                    for p in range(2):
                        if u == LAST_NORMS[p]:
                            layer_residual(b, L - 1, p)
                        if u == LAST_NORMS[p] + 2:
                            variance(b, 2 * L + p)
                        if u == NB - 4 + 2 * p:
                            last_relu(b, p)
                degrees(b + 1)
                assert steps[0] - before == STEPS_BATCH, (steps[0] - before)
            steps_before[0] = STEPS_BATCH * (B - 2)
            norms_to_layers(B - 1)
            for p in range(2):
                layer_residual(B - 1, L - 1, p)
                variance(B - 1, 2 * L + p)
                last_relu(B - 1, p)


_INS = ["x", "adj", "L0_gnn_U", "L0_gnn_w_scale", "L1_gnn_W", "L1_gnn_b", "L1_gnn_gamma", "L1_gnn_beta"]


def kernel(**inputs):
    import numpy as _np
    import concourse.bacc as _bacc
    from concourse import mybir as _mybir
    from concourse.bass_utils import run_bass_kernel_spmd as _run

    nc = _bacc.Bacc("TRN2", target_bir_lowering=False, num_devices=1, dynamic_dma_scratch_size=512)
    arrays, args = {}, []
    for name in _INS:
        a = _np.ascontiguousarray(inputs[name])
        if a.ndim == 0:
            a = a.reshape(1)
        arrays[f"in_{name}_dram"] = a
        args.append(nc.dram_tensor(f"in_{name}_dram", a.shape, _mybir.dt.from_np(a.dtype), kind="ExternalInput").ap())
    shape = inputs["x"].shape
    args.append(nc.dram_tensor("out_dram", shape, _mybir.dt.float32, kind="ExternalOutput").ap())
    adjacency_mixer_kernel(nc, *args)
    r = _run(nc, [arrays], core_ids=[0])
    return r.results[0]["out_dram"]
```

```python
import concourse.bass as bass
from concourse import mybir
from contextlib import ExitStack


def adjacency_mixer_kernel(nc, x, adj, U, w_scale, W, bias, gamma, beta, out):
    fp32 = mybir.dt.float32
    bf16 = mybir.dt.bfloat16
    ALU = mybir.AluOpType
    ACT = mybir.ActivationFunctionType
    AX = mybir.AxisListType

    B, N, C = x.shape
    R = U.shape[1]
    L = W.shape[0]
    P = 128
    T = N // P
    CH = 512
    NC = N // CH
    TC = CH // P
    HT = T // 2
    HC = HT * C
    DEG_EPS = 1e-12
    LN_EPS = 1e-5

    BUILD = [(j, c) for j in range(T) for c in range(j // TC + 1)]
    NB = len(BUILD)
    OUTS = 2 + 2 * L
    AFFINE = 4

    AIDED = [BUILD.index((j, 0)) for j in range(HT, T - 3)]

    def build_cols(j, c):
        return min((c + 1) * TC, j + 1) * P - c * CH

    def aided_before(u):
        return sum(v < u for v in AIDED)

    ORDER = []
    for u in range(NB + 1):
        if u < NB and u not in AIDED:
            ORDER.append(("sum", u))
        if u - 2 in AIDED:
            ORDER.append(("gate", u - 2))
        if u >= 1 and u - 1 not in AIDED:
            ORDER.append(("gate", u - 1))

    def strip(j):
        return j * (j + 1) // 2 * P

    def flipped(i, c):
        return list(range(max(TC * c, i + 1), TC * (c + 1)))

    FLIPS = [[(half, i, 2 * half + odd) for half in range(2) for i in range(T) if flipped(i, 2 * half + odd)]
             for odd in range(2)]
    NF = [len(f) for f in FLIPS]
    NF0 = [sum(half == 0 for half, _, _ in f) for f in FLIPS]

    TURNS = [min(2 * T, int(10 + 3 * min(u, TC) + 0.6 * min(max(u - TC, 0), 2 * TC) + 0.4 * max(u - 3 * TC, 0)))
             for u in range(NB + 1)]
    TURNED = TURNS.index(2 * T)
    LAST_OUTS = (TURNED - 1, TURNED + 1)
    LAST_LEAVES = (TURNED + 1, TURNED + 4)
    LAST_TAKEN = (TURNED, TURNED + 3)
    LAST_NORM = TURNED + 6
    HELD = 2
    RING = 4

    ctx = ExitStack()
    with ctx:
        def sb(name, shape, dt=fp32):
            return ctx.enter_context(nc.sbuf_tensor(name, shape, dt))

        def sem(name):
            return ctx.enter_context(nc.semaphore(name))

        Wt = sb("adjacency", [P, T, N])
        Kt = sb("k_lower", [P, strip(T)])
        ul = sb("u_left", [P, N], bf16)
        ur = sb("u_right", [P, N], bf16)
        xr = sb("x_residual", [P, T * C])
        hA = sb("h_a", [P, T * C])
        hB = sb("h_b", [P, T * C])
        G = sb("product_out", [P, CH])
        ident = sb("ident", [P, P])
        wl = sb("weights_twice", [P, L, 2 * C])
        bs = sb("bias_rows", [P, L, C])
        gs = sb("gamma_rows", [P, L, C])
        be = sb("beta_rows", [P, L, C])
        ws = sb("w_scale_col", [P, 1])
        ones = sb("ones", [P, 32])
        expo = sb("minus_half", [P, T])
        rows = sb("row_sums", [P, T, NC])
        deg = sb("degree", [P, T])
        dis = sb("degree_rsqrt", [P, T])
        dout = sb("degree_out", [P, T])
        rd = sb("norm_times_degree", [P, T])
        mean = sb("mean", [P, HT])
        var = sb("variance", [P, 2, HT])
        rstd = sb("rstd", [P, 2, HT])
        x_var = sb("x_variance", [P, T])
        x_rstd = sb("x_rstd", [P, T])

        cat = [Kt[:, m * T * P:(m + 1) * T * P].rearrange("p (t k) -> p t k", t=T) for m in range(2)]
        u_in = hA[:, 0:T * R].rearrange("p (t r) -> p t r", t=T)
        u_rest = [hA[:, (1 + m) * T * R:(2 + m) * T * R].rearrange("p (t r) -> p t r", t=T) for m in range(2)]
        u_part = [hB[:, m * T * R // 2:(m + 1) * T * R // 2].bitcast(bf16).rearrange("p (t r) -> p t r", t=T)
                  for m in range(3)]

        x_new = Kt[:, strip(T) - T * C:strip(T)]
        h1 = Kt[:, 0:T * C]

        def turned_slot(odd, v):
            if odd and v < NF0[1]:
                return G[:, :]
            return hA[:, odd * CH:(odd + 1) * CH]

        acc = ctx.enter_context(nc.psum_tensor("acc", [P, 2, CH], fp32))
        ring = ctx.enter_context(nc.psum_tensor("ring", [P, RING, CH], fp32))
        col = ctx.enter_context(nc.psum_tensor("column_sums", [P, CH], fp32))
        yps = ctx.enter_context(nc.psum_tensor("y_psum", [P, CH], fp32))

        w_in = [sem(f"strip_in_{j}") for j in range(T)]
        u_loaded = sem("u_loaded")
        const_in = sem("const_in")
        x_in = sem("x_in")
        xr_in = sem("xr_in")
        out_stored = sem("out_stored")
        wl_zeroed = sem("wl_zeroed")
        ident_made = sem("ident_made")
        ones_made = sem("ones_made")
        u_split = sem("u_split")
        u_turned = sem("u_turned")
        u_ready = sem("u_ready")
        gate_in = sem("gate_in")
        gated = sem("gated")
        turned_in = sem("turned_in")
        summed = sem("summed")
        aid_out = sem("aid_out")
        aid_summed = sem("aid_summed")
        k_made = sem("k_made")
        cols_summed = sem("cols_summed")
        cols_out = sem("cols_out")
        cols_turned = sem("cols_turned")
        deg_made = sem("deg_made")
        dis_made = sem("dis_made")
        dh_made = sem("dh_made")
        flip_in = [sem(f"flip_in_{side}") for side in ("even", "odd")]
        flip_out = [sem(f"flip_out_{side}") for side in ("even", "odd")]
        flip_used = [sem(f"flip_used_{side}") for side in ("even", "odd")]
        acc_done = sem("acc_done")
        g_out = sem("g_out")
        y_done = sem("y_done")
        x_centred = sem("x_centred")
        x_squared = sem("x_squared")
        x_var_made = sem("x_var_made")
        x_rstd_made = sem("x_rstd_made")
        x_moved = sem("x_moved")
        biased = sem("biased")
        y_taken = sem("y_taken")
        centred = sem("centred")
        squared = sem("squared")
        var_made = sem("var_made")
        rstd_made = sem("rstd_made")
        h_made = sem("h_made")
        strip_free = sem("strip_free")
        affine = sem("affine_step")
        affined = sem("affined")
        result = sem("result")
        step = sem("vector_step")

        def half(ap, p):
            return ap[:, p * HC:(p + 1) * HC]

        def tiles(ap):
            return ap.rearrange("p (t c) -> p t c", c=C)

        def over_c(ap):
            return ap.unsqueeze(2).broadcast_to([P, ap.shape[1], C])

        def over_t(ap):
            return ap.unsqueeze(1).broadcast_to([P, HT, C])

        reads = [h1, hA[:, :], hB[:, :]]
        writes = [hA[:, :], hB[:, :], hA[:, :]]

        block = ctx.enter_context(nc.Block())

        @block.sync
        def _(sp):
            def load_x(b, dst, loaded):
                sp.dma_start(tiles(dst), x[b].rearrange("(t p) c -> p t c", p=P)).then_inc(loaded, 16)

            def load_strip(b, j):
                sp.dma_start(Wt[:, j, :], adj[b, j * P:(j + 1) * P, :]).then_inc(w_in[j], 16)

            sp.dma_start(u_in, U.rearrange("(t p) r -> p t r", p=P)).then_inc(u_loaded, 16)
            load_x(0, x_new, x_in)
            load_strip(0, 0)
            for q in range(2):
                sp.wait_ge(wl_zeroed, 1)
                sp.dma_start(wl[q * C:(q + 1) * C, :, q * C:(q + 1) * C], W.rearrange("l d e -> d l e")).then_inc(const_in, 16)
            for rows_sb, src in ((bs, bias), (gs, gamma), (be, beta)):
                sp.dma_start(rows_sb[:, :, :], src.partition_broadcast(P)).then_inc(const_in, 16)
            sp.dma_start(ws[:, :], w_scale.partition_broadcast(P)).then_inc(const_in, 16)
            load_x(0, xr[:, :], xr_in)
            for j in range(1, T):
                load_strip(0, j)

            def store(b):
                sp.wait_ge(result, 2 * b + 2)
                sp.dma_start(out[b].rearrange("(t p) c -> p t c", p=P), tiles(xr[:, :])).then_inc(out_stored, 16)

            with sp.Fori(0, B - 1) as b:
                sp.wait_ge(centred, OUTS * b + 2)
                load_x(b + 1, x_new, x_in)
                for j in range(T):
                    if j < T - 1:
                        sp.wait_ge(strip_free, (T - 1) * b + j + 1)
                    else:
                        sp.wait_ge(acc_done, OUTS * (b + 1))
                    load_strip(b + 1, j)
                store(b)
                sp.wait_ge(out_stored, 16 * (b + 1))
                load_x(b + 1, xr[:, :], xr_in)
            by_half = out[B - 1].rearrange("(h t p) c -> h p t c", h=2, p=P)
            for p in range(2):
                sp.wait_ge(result, 2 * (B - 1) + p + 1)
                sp.dma_start(by_half[p], tiles(half(xr, p))).then_inc(out_stored, 16)
            sp.wait_ge(out_stored, 16 * (B + 1))

        @block.tensor
        def _(pe):
            def product(bank, h, j, c):
                o = C * (c % 2)
                return nc.tensor.matmul(acc[o:o + C, bank, :], h[:, j * C:(j + 1) * C],
                                        Wt[:, j, c * CH:(c + 1) * CH], start=(j == 0), stop=(j == T - 1))

            def layer_step(b, l, j, halves=(0, 1)):
                for p in halves:
                    if j == 0:
                        pe.wait_ge(g_out, OUTS * b + 2 * l + p + 1)
                    if j % HT == 0:
                        pe.wait_ge(h_made, 2 * L * b + 2 * l + j // HT + 1)
                    for c in (2 * p, 2 * p + 1):
                        m = product(p, reads[l], j, c)
                    if j == T - 1:
                        m.then_inc(acc_done, 1)
                return m

            def leave(b, n):
                pe.wait_ge(g_out, OUTS * b + n + 1)
                if n == 2 * L + 1 and not isinstance(b, int):
                    pe.wait_ge(y_taken, 2 * b + 1)
                elif n > 0 or not isinstance(b, int):
                    pe.wait_ge(var_made, OUTS * b + n)
                by_chunk = yps[:, :].rearrange("p (a k c) -> p a k c", a=2, c=C)
                for k in range(TC):
                    if n < 2:
                        m = nc.tensor.transpose(by_chunk[:, :, k, :], G[:, k * P:(k + 1) * P], ident[:, :])
                    else:
                        m = nc.tensor.matmul(by_chunk[:, :, k, :], G[:, k * P:(k + 1) * P], wl[:, (n - 2) // 2, :],
                                             start=True, stop=True)
                m.then_inc(y_done, 1)

            def build_transposes(b, u):
                j, c = BUILD[u]
                if c == 0:
                    pe.wait_ge(w_in[j], 16 * (b + 1))
                if u == 0:
                    pe.wait_ge(x_var_made, 2 * b + 2)
                if u - 2 in AIDED:
                    pe.wait_ge(aid_out, len(AIDED) * b + aided_before(u - 2) + 1)
                elif u >= 2:
                    pe.wait_ge(summed, (NB - len(AIDED)) * b + u - 2 - aided_before(u - 2) + 1)
                for k in range(build_cols(j, c) // P):
                    m = nc.tensor.transpose(ring[:, 2 + u % 2, k * P:(k + 1) * P],
                                            Wt[:, c * TC + k, j * P:(j + 1) * P], ident[:, :])
                m.then_inc(turned_in, 1)

            def build_gate(b, u):
                j, c = BUILD[u]
                n = build_cols(j, c)
                if u >= 2:
                    pe.wait_ge(k_made, NB * b + u - 1)
                nc.tensor.matmul(ring[:, u % 2, 0:n], ul[:, j * P:(j + 1) * P], ur[:, c * CH:c * CH + n],
                                 start=True, stop=True).then_inc(gate_in, 1)

            def column_sums(b, j):
                by_tile = Kt[:, strip(j):strip(j) + j * P].rearrange("p (t n) -> p t n", n=P)
                pe.wait_ge(k_made, NB * b + BUILD.index((j, j // TC)) + 1)
                for q in range(min(TC, j)):
                    n = (j - 1 - q) // TC + 1
                    nc.tensor.matmul(col[32 * q:32 * q + 32, 0:n * P], ones[:, :], by_tile[:, q:j:TC, :],
                                     start=(j == q + 1), stop=False, skip_group_check=True)

            def last_column_sums(b, c):
                j = T - 1
                pe.wait_ge(k_made, NB * b + BUILD.index((j, c)) + 1)
                for q in range(TC if c < NC - 1 else TC - 1):
                    at = strip(j) + c * CH + q * P
                    m = nc.tensor.matmul(col[32 * q:32 * q + 32, c * P:(c + 1) * P], ones[:, :], Kt[:, at:at + P],
                                         start=False, stop=True, skip_group_check=True)
                return m

            def column_sums_after(b, u):
                if u >= 0:
                    j, c = BUILD[u]
                    if 0 < j < T - 1 and c == j // TC:
                        column_sums(b, j)

            def build_tail(b):
                for c in range(NC - 1):
                    m = last_column_sums(b, c)
                m.then_inc(cols_summed, 1)
                pe.wait_ge(cols_out, 2 * b + 1)
                for k in range(NC - 1):
                    nc.tensor.transpose(acc[:, 1, k * P:(k + 1) * P], G[:, k * P:(k + 1) * P], ident[:, :])
                last_column_sums(b, NC - 1).then_inc(cols_summed, 1)
                flip(b, 0, 0)
                pe.wait_ge(cols_out, 2 * b + 2)
                nc.tensor.transpose(acc[:, 1, CH - P:CH - 32], G[0:P - 32, CH - P:CH], ident[0:P - 32, 0:P - 32])\
                  .then_inc(cols_turned, 1)

            def flip(b, p, i):
                for odd in range(2):
                    c = 2 * p + odd
                    if (p, i, c) not in FLIPS[odd]:
                        continue
                    v = FLIPS[odd].index((p, i, c))
                    if v == 0:
                        pe.wait_ge(k_made, NB * (b + 1))
                    if v >= 2:
                        pe.wait_ge(flip_out[odd], NF[odd] * b + v - 1)
                    for k, j in enumerate(flipped(i, c)):
                        m = nc.tensor.transpose(ring[:, 2 * odd + v % 2, k * P:(k + 1) * P],
                                                Kt[:, strip(j) + i * P:strip(j) + (i + 1) * P], ident[:, :])
                    m.then_inc(flip_in[odd], 1)

            def k_product(b):
                for p in range(2):
                    for i in range(T):
                        if i + 1 < T:
                            flip(b, p, i + 1)
                        elif p == 0:
                            flip(b, 1, 0)
                        if p == 0 and i % TC == 0:
                            pe.wait_ge(dh_made, NC * b + i // TC + 1)
                        dh = hB[:, i * C:(i + 1) * C]
                        for odd in range(2):
                            c, o = 2 * p + odd, C * odd
                            if TC * c <= i:
                                n = min(CH, (i + 1) * P - c * CH)
                                m = nc.tensor.matmul(acc[o:o + C, p, 0:n], dh,
                                                     Kt[:, strip(i) + c * CH:strip(i) + c * CH + n],
                                                     start=(i == 0), stop=(i == T - 1), skip_group_check=True)
                        if i == T - 1:
                            m.then_inc(acc_done, 1)
                        for odd in range(2):
                            c, o = 2 * p + odd, C * odd
                            if (p, i, c) in FLIPS[odd]:
                                v = FLIPS[odd].index((p, i, c))
                                lo = flipped(i, c)[0] * P - c * CH
                                pe.wait_ge(flip_out[odd], NF[odd] * b + v + 1)
                                nc.tensor.matmul(acc[o:o + C, p, lo:CH], dh, turned_slot(odd, v)[:, 0:CH - lo],
                                                 start=(i == 0 and c > 0), stop=False, skip_group_check=True)\
                                  .then_inc(flip_used[odd], 1)
                        if p == 1 and i == 2:
                            leave(b, 0)

            def full_layer(b, l):
                for p, steps in ((0, range(0, 8)), (1, range(0, 4)), (0, range(8, 16)), (1, range(4, 16))):
                    for j in steps:
                        layer_step(b, l, j, (p,))
                        if (p, j) == (0, 1):
                            leave(b, 2 * l + 1)
                        if (p, j) == (1, 5):
                            leave(b, 2 * l + 2)

            def last_layer_turn(b, k):
                j, p = k // 2, k % 2
                if k < 2 * HELD:
                    p, j = divmod(k, HELD)
                if k == HELD:
                    leave(b, 2 * L - 1)
                m = layer_step(b, L - 1, j, (p,))
                if p == 1 and j < T - 1:
                    m.then_inc(strip_free, 1)

            def window(b):
                turn = 0
                for u in range(NB + 1):
                    turns = TURNS[u]
                    while turn < turns - 1:
                        last_layer_turn(b, turn)
                        turn += 1
                    if u < NB:
                        build_transposes(b + 1, u)
                    while turn < turns:
                        last_layer_turn(b, turn)
                        turn += 1
                    if u > 0:
                        build_gate(b + 1, u - 1)
                        column_sums_after(b + 1, u - 3)
                    for p in range(2):
                        if u == LAST_LEAVES[p]:
                            leave(b, 2 * L + p)
                column_sums_after(b + 1, NB - 2)
                build_tail(b + 1)

            pe.wait_ge(ident_made, 2)
            for m in range(2):
                pe.wait_ge(u_split, m + 1)
                for q in range(NC):
                    if m == 1:
                        pe.wait_ge(u_ready, q + 1)
                    for k in range(TC):
                        t = nc.tensor.transpose(ring[:, q, k * P:(k + 1) * P], cat[m][:, q * TC + k, :], ident[:, :])
                    t.then_inc(u_turned, 1)
            pe.wait_ge(u_ready, 2 * NC)
            pe.wait_ge(ones_made, 1)
            for u in range(NB + 1):
                if u < NB:
                    build_transposes(0, u)
                if u > 0:
                    build_gate(0, u - 1)
                    column_sums_after(0, u - 3)
            column_sums_after(0, NB - 2)
            build_tail(0)

            k_product(0)
            with pe.Fori(0, B - 1) as b:
                for l in range(L - 1):
                    full_layer(b, l)
                window(b)
                k_product(b + 1)
            for l in range(L):
                full_layer(B - 1, l)
            leave(B - 1, 2 * L + 1)

        @block.scalar
        def _(act):
            def gate(b, u):
                j, c = BUILD[u]
                n = build_cols(j, c)
                act.wait_ge(gate_in, NB * b + u + 1)
                nc.scalar.activation(ring[:, u % 2, 0:n], ring[:, u % 2, 0:n], ACT.Sigmoid).then_inc(gated, 1)

            def aid(b, u):
                if u in AIDED:
                    j, c = BUILD[u]
                    at, n = strip(j) + c * CH, build_cols(j, c)
                    act.wait_ge(turned_in, NB * b + u + 1)
                    nc.scalar.activation(Kt[:, at:at + n], ring[:, 2 + u % 2, 0:n], ACT.Copy).then_inc(aid_out, 1)

            def square(b, n, src):
                act.wait_ge(centred, OUTS * b + n + 1)
                if n == 2 * L and not isinstance(b, int):
                    act.wait_ge(y_taken, 2 * b + 2)
                elif n > 0:
                    act.wait_ge(var_made, OUTS * b + n)
                nc.scalar.activation(yps[:, :], src, ACT.Square).then_inc(squared, 1)

            def square_x(b, p):
                act.wait_ge(x_centred, 2 * b + p + 1)
                nc.scalar.activation(ring[:, 2 + p, :], half(x_new, p), ACT.Square).then_inc(x_squared, 1)

            def move_x(b, p):
                act.wait_ge(x_centred, 2 * b + 2)
                if not isinstance(b, int):
                    act.wait_ge(y_taken, 2 * b)
                nc.scalar.activation(half(hB, p), half(x_new, p), ACT.Relu).then_inc(x_moved, 1)

            def product_out(b, n):
                act.wait_ge(acc_done, OUTS * b + n + 1)
                if n == 0:
                    act.wait_ge(cols_turned, b + 1)
                else:
                    act.wait_ge(y_done, OUTS * b + n)
                nc.scalar.activation(G[:, :], acc[:, n % 2, :], ACT.Copy).then_inc(g_out, 1)

            def cols_to_sbuf(b):
                act.wait_ge(cols_summed, 2 * b + 1)
                if not isinstance(b, int):
                    act.wait_ge(y_done, OUTS * b)
                nc.scalar.activation(G[:, 0:CH - P], col[:, 0:CH - P], ACT.Copy).then_inc(cols_out, 1)
                act.wait_ge(cols_summed, 2 * b + 2)
                nc.scalar.activation(G[0:96, CH - P:CH], col[0:96, CH - P:CH], ACT.Copy).then_inc(cols_out, 1)

            def flip_to_sbuf(b, v):
                _, i, c = FLIPS[0][v]
                n = len(flipped(i, c)) * P
                act.wait_ge(flip_in[0], NF[0] * b + v + 1)
                if v > 0:
                    act.wait_ge(flip_used[0], NF[0] * b + v)
                elif not isinstance(b, int):
                    act.wait_ge(result, 2 * b - 1)
                nc.scalar.activation(turned_slot(0, v)[:, 0:n], ring[:, v % 2, 0:n], ACT.Copy).then_inc(flip_out[0], 1)

            def k_product(b):
                for v in range(NF[0]):
                    flip_to_sbuf(b, v)
                    if v == NF0[0] - 1 and not isinstance(b, int):
                        square(b - 1, 2 * L + 1, half(writes[L - 1], 1))
                    if v == NF0[0]:
                        product_out(b, 0)
                    if v == NF0[0] + 6:
                        square(b, 0, half(h1, 0))
                product_out(b, 1)
                square(b, 1, half(h1, 1))

            def full_layers(b):
                for l in range(L if isinstance(b, int) else L - 1):
                    for p in range(2):
                        product_out(b, 2 + 2 * l + p)
                        square(b, 2 + 2 * l + p, half(writes[l], p))
                        if (l, p) == (0, 1) and not isinstance(b, int):
                            square_x(b + 1, 0)
                            square_x(b + 1, 1)

            square_x(0, 0)
            square_x(0, 1)
            for u in range(NB):
                aid(0, u + 1)
                gate(0, u)
                if u in (4, 5):
                    move_x(0, u - 4)
            cols_to_sbuf(0)
            k_product(0)
            with act.Fori(0, B - 1) as b:
                full_layers(b)
                for u in range(NB):
                    aid(b + 1, u + 1)
                    gate(b + 1, u)
                    for p in range(2):
                        if u == LAST_OUTS[p]:
                            product_out(b, 2 * L + p)
                    if u in (LAST_TAKEN[1] + 2, LAST_TAKEN[1] + 3):
                        move_x(b + 1, u - LAST_TAKEN[1] - 2)
                    if u == LAST_NORM + 2:
                        square(b, 2 * L, half(writes[L - 1], 0))
                cols_to_sbuf(b + 1)
                k_product(b + 1)
            full_layers(B - 1)

        @block.gpsimd
        def _(pool):
            pool.memset(wl[:, :, :], 0.0).then_inc(wl_zeroed, 1)
            pool.memset(ident[:, :], 0.0).then_inc(ident_made, 1)
            pool.wait_ge(ident_made, 1)
            pool.affine_select(out=ident[:, :], in_=ident[:, :], compare_op=ALU.not_equal, fill=1.0,
                               base=0, pattern=[[-1, P]], channel_multiplier=1).then_inc(ident_made, 1)
            pool.wait_ge(ones_made, 1)

            def root(b, n):
                pool.wait_ge(var_made, OUTS * b + n + 1)
                nc.gpsimd.tensor_tensor(rstd[:, n % 2, :], var[:, n % 2, :], expo[:, 0:HT], ALU.pow).then_inc(rstd_made, 1)

            def degree_root(b, q):
                pool.wait_ge(deg_made, b + 1)
                mine = slice(q * TC, (q + 1) * TC)
                nc.gpsimd.tensor_tensor(dis[:, mine], deg[:, mine], expo[:, 0:TC], ALU.pow).then_inc(dis_made, 1)

            def last_bias(b):
                pool.wait_ge(acc_done, OUTS * (b + 1))
                for p in range(2):
                    src = tiles(half(reads[L - 1], p))
                    nc.gpsimd.tensor_tensor(src, src, over_t(bs[:, L - 1, :]), ALU.add).then_inc(biased, 1)

            def aid(b):
                for u in range(NB):
                    if u == TURNED and not isinstance(b, int):
                        last_bias(b - 1)
                    if u not in AIDED:
                        continue
                    j, c = BUILD[u]
                    at, n = strip(j) + c * CH, build_cols(j, c)
                    pool.wait_ge(w_in[j], 16 * (b + 1))
                    pool.wait_ge(aid_out, len(AIDED) * b + aided_before(u) + 1)
                    nc.gpsimd.tensor_tensor(Kt[:, at:at + n], Kt[:, at:at + n], Wt[:, j, c * CH:c * CH + n], ALU.add)\
                      .then_inc(aid_summed, 1)

            def last_affine(b, p):
                dst = half(writes[L - 1], p)
                n = 2 * L + p
                a = AFFINE * b + 2 * p
                pool.wait_ge(squared, OUTS * b + n + 1)
                nc.gpsimd.tensor_tensor(tiles(dst), tiles(dst), over_t(gs[:, L - 1, :]), ALU.mult).then_inc(affine, 1)
                root(b, n)
                pool.wait_ge(rstd_made, OUTS * b + n + 1)
                pool.wait_ge(affine, a + 1)
                nc.gpsimd.tensor_tensor(tiles(dst), tiles(dst), over_c(rstd[:, p, :]), ALU.mult).then_inc(affine, 1)
                pool.wait_ge(affine, a + 2)
                nc.gpsimd.tensor_tensor(tiles(dst), tiles(dst), over_t(be[:, L - 1, :]), ALU.add).then_inc(affined, 1)

            def x_root(b):
                for p in range(2):
                    mine = slice(p * HT, (p + 1) * HT)
                    pool.wait_ge(x_var_made, 2 * b + p + 1)
                    nc.gpsimd.tensor_tensor(x_rstd[:, mine], x_var[:, mine], expo[:, 0:HT], ALU.pow)\
                      .then_inc(x_rstd_made, 1)

            def k_product_roots(b):
                for q in range(NC):
                    degree_root(b, q)
                if not isinstance(b, int):
                    last_affine(b - 1, 1)
                for n in range(2):
                    root(b, n)

            def layer_roots(b):
                for n in range(2, 2 * L):
                    root(b, n)
                    if n == 3 and not isinstance(b, int):
                        x_root(b + 1)
                if isinstance(b, int):
                    for n in range(2 * L, 2 * L + 2):
                        root(b, n)
                else:
                    aid(b + 1)
                    last_affine(b, 0)

            x_root(0)
            aid(0)
            k_product_roots(0)
            with pool.Fori(0, B - 1) as b:
                layer_roots(b)
                k_product_roots(b + 1)
            layer_roots(B - 1)

        STEPS_BATCH = 51

        @block.vector
        def _(dve):
            steps = [0]
            steps_before = [0]

            def link(instruction):
                steps[0] += 1
                instruction.then_inc(step, 1)
                dve.wait_ge(step, steps[0] + steps_before[0])

            def add_transposed(b, u):
                j, c = BUILD[u]
                n = build_cols(j, c)
                at = strip(j) + c * CH
                dve.wait_ge(w_in[j], 16 * (b + 1))
                dve.wait_ge(turned_in, NB * b + u + 1)
                if (j, c) == (T - 1, NC // 2):
                    dve.wait_ge(x_moved, 2 * b + 2)
                nc.vector.tensor_tensor(Kt[:, at:at + n], Wt[:, j, c * CH:c * CH + n], ring[:, 2 + u % 2, 0:n],
                                        ALU.add).then_inc(summed, 1)

            def times_gate(b, u):
                j, c = BUILD[u]
                n = build_cols(j, c)
                at = strip(j) + c * CH
                if u in AIDED:
                    dve.wait_ge(aid_summed, len(AIDED) * b + aided_before(u) + 1)
                else:
                    dve.wait_ge(summed, (NB - len(AIDED)) * b + u - aided_before(u) + 1)
                dve.wait_ge(gated, NB * b + u + 1)
                nc.vector.scalar_tensor_tensor(out=Kt[:, at:at + n], in0=Kt[:, at:at + n], scalar=1.0,
                                               in1=ring[:, u % 2, 0:n], op0=ALU.mult, op1=ALU.mult,
                                               accum_out=rows[:, j, c:c + 1]).then_inc(k_made, 1)

            def centre(src, dst, done):
                link(nc.vector.tensor_reduce(mean[:, :], tiles(src), AX.X, ALU.add))
                nc.vector.scalar_tensor_tensor(out=tiles(dst), in0=over_c(mean[:, :]), scalar=-1.0 / C, in1=tiles(src),
                                               op0=ALU.mult, op1=ALU.add).then_inc(done, 1)

            def variance(b, n):
                dve.wait_ge(squared, OUTS * b + n + 1)
                link(nc.vector.tensor_reduce(var[:, n % 2, :], tiles(yps[:, :]), AX.X, ALU.add))
                nc.vector.tensor_scalar(var[:, n % 2, :], var[:, n % 2, :], 1.0 / C, LN_EPS, ALU.mult, ALU.add)\
                  .then_inc(var_made, 1)

            def x_norm(b):
                dve.wait_ge(x_in, 16 * (b + 1))
                for p in range(2):
                    if p > 0:
                        dve.wait_ge(x_centred, 2 * b + 1)
                    centre(half(x_new, p), half(x_new, p), x_centred)
                for p in range(2):
                    mine = slice(p * HT, (p + 1) * HT)
                    dve.wait_ge(x_squared, 2 * b + p + 1)
                    link(nc.vector.tensor_reduce(x_var[:, mine], tiles(ring[:, 2 + p, :]), AX.X, ALU.add))
                    nc.vector.tensor_scalar(x_var[:, mine], x_var[:, mine], 1.0 / C, LN_EPS, ALU.mult, ALU.add)\
                      .then_inc(x_var_made, 1)

            def degrees(b):
                dve.wait_ge(k_made, NB * (b + 1))
                link(nc.vector.tensor_reduce(deg[:, :], rows[:, :, :], AX.X, ALU.add))
                dve.wait_ge(cols_turned, b + 1)
                link(nc.vector.tensor_tensor(deg[:, 0:T - 1], deg[:, 0:T - 1], acc[:, 1, 0:32 * (T - 2) + 1:32], ALU.add))
                nc.vector.tensor_scalar(deg[:, :], deg[:, :], 0.5, DEG_EPS, ALU.mult, ALU.max).then_inc(deg_made, 1)
                if not isinstance(b, int):
                    last_relu(b - 1, 0)
                dve.wait_ge(x_rstd_made, 2 * b + 2)
                dve.wait_ge(x_moved, 2 * b + 2)

            def times_degree(b, q):
                dve.wait_ge(dis_made, NC * b + q + 1)
                mine = slice(q * TC, (q + 1) * TC)
                link(nc.vector.tensor_tensor(rd[:, mine], dis[:, mine], x_rstd[:, mine], ALU.mult))
                h = tiles(hB[:, q * TC * C:(q + 1) * TC * C])
                nc.vector.tensor_tensor(h, h, over_c(rd[:, mine]), ALU.mult).then_inc(dh_made, 1)

            def flip_to_sbuf(b, v):
                _, i, c = FLIPS[1][v]
                n = len(flipped(i, c)) * P
                dve.wait_ge(flip_in[1], NF[1] * b + v + 1)
                if v > 0:
                    dve.wait_ge(flip_used[1], NF[1] * b + v)
                nc.vector.tensor_copy(turned_slot(1, v)[:, 0:n], ring[:, 2 + v % 2, 0:n]).then_inc(flip_out[1], 1)

            def first_residual(b, p):
                dve.wait_ge(y_done, OUTS * b + p + 1)
                ys, xs, hs = tiles(yps[:, :]), half(xr, p), half(h1, p)
                link(nc.vector.tensor_tensor(ys, ys, over_c(dout[:, p * HT:(p + 1) * HT]), ALU.mult))
                dve.wait_ge(xr_in, 16 * (b + 1))
                link(nc.vector.tensor_tensor(xs, yps[:, :], xs, ALU.add))
                centre(xs, hs, centred)

            def first_relu(b, p):
                hs = half(h1, p)
                dve.wait_ge(rstd_made, OUTS * b + 1 + p)
                nc.vector.scalar_tensor_tensor(out=tiles(hs), in0=tiles(hs), scalar=0.0,
                                               in1=over_c(rstd[:, p, :]), op0=ALU.max, op1=ALU.mult).then_inc(h_made, 1)

            def layer_residual(b, l, p):
                src, dst = half(reads[l], p), half(writes[l], p)
                dve.wait_ge(y_done, OUTS * b + 3 + 2 * l + p)
                link(nc.vector.tensor_tensor(dst, yps[:, :], src, ALU.add))
                link(nc.vector.tensor_tensor(tiles(dst), tiles(dst), over_t(bs[:, l, :]), ALU.add))
                centre(dst, dst, centred)

            def last_taken(b, p):
                dve.wait_ge(y_done, OUTS * b + 2 * L + p + 1)
                dve.wait_ge(biased, 2 * b + p + 1)
                nc.vector.tensor_tensor(half(writes[L - 1], p), yps[:, :], half(reads[L - 1], p), ALU.add)\
                  .then_inc(y_taken, 1)

            def last_centre(b, p):
                dst = half(writes[L - 1], p)
                dve.wait_ge(y_taken, 2 * b + p + 1)
                if p == 1:
                    dve.wait_ge(centred, OUTS * b + 2 * L + 1)
                centre(dst, dst, centred)

            def layer_relu(b, l, p):
                dst = half(writes[l], p)
                link(nc.vector.tensor_tensor(tiles(dst), tiles(dst), over_t(gs[:, l, :]), ALU.mult))
                dve.wait_ge(rstd_made, OUTS * b + 3 + 2 * l + p)
                link(nc.vector.tensor_tensor(tiles(dst), tiles(dst), over_c(rstd[:, p, :]), ALU.mult))
                link(nc.vector.tensor_tensor(tiles(dst), tiles(dst), over_t(be[:, l, :]), ALU.add))
                if l < L - 1:
                    nc.vector.tensor_scalar(dst, dst, 0.0, None, ALU.max).then_inc(h_made, 1)
                else:
                    x_plus_relu(p)

            def x_plus_relu(p):
                nc.vector.scalar_tensor_tensor(out=half(xr, p), in0=half(writes[L - 1], p), scalar=0.0, in1=half(xr, p),
                                               op0=ALU.max, op1=ALU.add).then_inc(result, 1)

            def last_relu(b, p):
                dve.wait_ge(affined, 2 * b + p + 1)
                x_plus_relu(p)

            def k_product(b):
                times_degree(b, 0)
                for v in range(NF[1]):
                    if v == NF0[1] and not isinstance(b, int):
                        last_relu(b - 1, 1)
                        dve.wait_ge(result, 2 * b)
                    flip_to_sbuf(b, v)
                    if v < NC - 1:
                        times_degree(b, v + 1)
                    if v == NC - 1:
                        link(nc.vector.tensor_scalar(dout[:, :], dis[:, :], ws[:, 0:1], 0.5, ALU.mult, ALU.mult))
                    if not isinstance(b, int):
                        if v == 3:
                            last_centre(b - 1, 1)
                        if v == 5:
                            variance(b - 1, 2 * L + 1)
                    if v == NF0[1] + 4:
                        first_residual(b, 0)
                    if v == NF0[1] + 6:
                        variance(b, 0)
                    if v == NF0[1] + 7:
                        first_relu(b, 0)
                first_residual(b, 1)
                variance(b, 1)
                first_relu(b, 1)

            def full_layers(b):
                for l in range(L if isinstance(b, int) else L - 1):
                    for p in range(2):
                        layer_residual(b, l, p)
                        variance(b, 2 + 2 * l + p)
                        layer_relu(b, l, p)
                        if (l, p) == (0, 1) and not isinstance(b, int):
                            x_norm(b + 1)

            dve.wait_ge(u_loaded, 16)
            parts_l = (0, 0, 1, 1, 0, 2, 1, 2)
            parts_r = (0, 1, 0, 1, 2, 0, 2, 1)
            nc.vector.memset(expo[:, :], -0.5)
            nc.vector.memset(rows[:, :, :], 0.0)
            nc.vector.memset(ones[:, :], 1.0).then_inc(ones_made, 1)
            rest = u_in
            for m in range(3):
                link(nc.vector.tensor_copy(u_part[m], rest))
                if m < 2:
                    link(nc.vector.tensor_tensor(u_rest[m], rest, u_part[m], ALU.subtract))
                    rest = u_rest[m]
            for side, parts in enumerate((parts_l, parts_r)):
                for q, m in enumerate(parts):
                    i = nc.vector.tensor_copy(cat[side][:, :, q * R:(q + 1) * R], u_part[m])
                i.then_inc(u_split, 1)
            for side, dst in enumerate((ul, ur)):
                for q in range(NC):
                    dve.wait_ge(u_turned, side * NC + q + 1)
                    nc.vector.tensor_copy(dst[:, q * CH:(q + 1) * CH], ring[:, q, :]).then_inc(u_ready, 1)
            dve.wait_ge(const_in, 16 * 6)
            x_norm(0)
            for kind, u in ORDER:
                if kind == "sum":
                    add_transposed(0, u)
                else:
                    times_gate(0, u)
            degrees(0)
            k_product(0)
            before = steps[0]

            with dve.Fori(0, B - 1) as b:
                steps_before[0] = STEPS_BATCH * b
                full_layers(b)
                for kind, u in ORDER:
                    if kind == "sum":
                        add_transposed(b + 1, u)
                        continue
                    times_gate(b + 1, u)
                    for p in range(2):
                        if u == LAST_TAKEN[p]:
                            last_taken(b, p)
                    if u == LAST_NORM - 1:
                        last_centre(b, 0)
                    if u == LAST_NORM + 2:
                        variance(b, 2 * L)
                degrees(b + 1)
                k_product(b + 1)
                assert steps[0] - before == STEPS_BATCH, (steps[0] - before)
            steps_before[0] = STEPS_BATCH * (B - 2)
            full_layers(B - 1)


_INS = ["x", "adj", "L0_gnn_U", "L0_gnn_w_scale", "L1_gnn_W", "L1_gnn_b", "L1_gnn_gamma", "L1_gnn_beta"]


def kernel(**inputs):
    import numpy as _np
    import concourse.bacc as _bacc
    from concourse import mybir as _mybir
    from concourse.bass_utils import run_bass_kernel_spmd as _run

    nc = _bacc.Bacc("TRN2", target_bir_lowering=False, num_devices=1, dynamic_dma_scratch_size=512)
    arrays, args = {}, []
    for name in _INS:
        a = _np.ascontiguousarray(inputs[name])
        if a.ndim == 0:
            a = a.reshape(1)
        arrays[f"in_{name}_dram"] = a
        args.append(nc.dram_tensor(f"in_{name}_dram", a.shape, _mybir.dt.from_np(a.dtype), kind="ExternalInput").ap())
    shape = inputs["x"].shape
    args.append(nc.dram_tensor("out_dram", shape, _mybir.dt.float32, kind="ExternalOutput").ap())
    adjacency_mixer_kernel(nc, *args)
    r = _run(nc, [arrays], core_ids=[0])
    return r.results[0]["out_dram"]
```
